# Optimizing a Trainium2 kernel written in Bass

```python
import numpy as np
import jax
import jax.numpy as jnp

def _softmax(x, axis=-1):
    return jax.nn.softmax(x, axis=axis)

def _gelu(x):
    return jax.nn.gelu(x, approximate=True)

def _silu(x):
    return jax.nn.silu(x)

def _sigmoid(x):
    return jax.nn.sigmoid(x)

def _layernorm(x, axis=-1, eps=1e-05):
    m = jnp.mean(x, axis=axis, keepdims=True)
    v = jnp.var(x, axis=axis, keepdims=True)
    return (x - m) / jnp.sqrt(v + eps)

def _scatter_add(tgt, idx, src, axis=0):
    return tgt.at[idx].add(src)

def _segment_sum(src, seg, n):
    return jax.ops.segment_sum(src, seg, n)
kernel_name = 'mk_adj_ffn_d1_adj_r2_d6c613'

def setup_inputs(seed: int=0):
    np.random.seed(seed)
    _w = jnp.asarray

    def _rec_inputs():
        import jax
        import jax.numpy as jnp
        _gk = jax.random.key(seed)
        x = -0.0002928 + 1 * jax.random.normal(jax.random.fold_in(_gk, 1), (8192, 256), jnp.float32)
        _a = jax.random.bernoulli(jax.random.fold_in(_gk, 2), 0.000976562, (8192, 8192))
        _a = jnp.logical_or(_a, jnp.swapaxes(_a, -1, -2))
        _a = jnp.logical_or(_a, jnp.eye(8192, dtype=bool))
        _af = _a.astype(jnp.float32)
        _af = _af * jax.random.uniform(jax.random.fold_in(_gk, 3), (8192, 8192), jnp.float32, 0.05, 1)
        adj = _af
        return (x, adj)
    x, adj = _rec_inputs()

    def _L0_gnn_setup():
        import jax, jax.numpy as jnp
        import numpy as np
        N = 4096
        F_IN = 256
        F_OUT = 256
        key = jax.random.key(seed)
        k1, k2, k3, k4 = jax.random.split(key, 4)
        stdv = 1.0 / np.sqrt(F_OUT)
        inp = jax.random.normal(k1, (N, F_IN), dtype=jnp.float32)
        adj = jax.random.uniform(k2, (N, N), dtype=jnp.float32)
        weight = jax.random.uniform(k3, (F_IN, F_OUT), minval=-stdv, maxval=stdv, dtype=jnp.float32)
        bias = jax.random.uniform(k4, (F_OUT,), minval=-stdv, maxval=stdv, dtype=jnp.float32)
        return {'inp': inp, 'adj': adj, 'weight': weight, 'bias': bias}
    _L0_gnn_all = _L0_gnn_setup()
    _L0_gnn_in = {k: v for k, v in _L0_gnn_all.items() if k in ('weight', 'bias')}
    del _L0_gnn_all

    def _L0_ffn_setup():
        import jax, jax.numpy as jnp
        import numpy as np
        D_MODEL, D_STATE, D_CONV, D_INPUT, D_OUTPUT = (512, 16, 4, 256, 256)
        EXPAND = 2
        D_INNER = EXPAND * D_MODEL
        DT_RANK = (D_MODEL + 15) // 16
        B, L = (4, 1024)

        def _mamba(x, W_in, conv_w, conv_b, W_xproj, W_dt, b_dt, A_log, Dp, W_out):
            xz = jnp.einsum('bld,ed->ble', x, W_in)
            u, z = jnp.split(xz, 2, axis=-1)
            u_pad = jnp.pad(u, ((0, 0), (D_CONV - 1, 0), (0, 0)))
            u = sum((u_pad[:, k:k + u.shape[1], :] * conv_w[:, k] for k in range(D_CONV))) + conv_b
            u = jax.nn.silu(u)
            dbc = jnp.einsum('bld,ed->ble', u, W_xproj)
            dt, B_ssm, C_ssm = jnp.split(dbc, [DT_RANK, DT_RANK + D_STATE], axis=-1)
            delta = jax.nn.softplus(jnp.einsum('blr,dr->bld', dt, W_dt) + b_dt)
            A = -jnp.exp(A_log)

            def step(h, ins):
                d_t, B_t, C_t, u_t = ins
                dA = jnp.exp(d_t[..., None] * A)
                h = dA * h + (d_t * u_t)[..., None] * B_t[:, None, :]
                y_t = jnp.einsum('bds,bs->bd', h, C_t)
                return (h, y_t)
            h0 = jnp.zeros((u.shape[0], D_INNER, D_STATE), u.dtype)
            xs = (delta.transpose(1, 0, 2), B_ssm.transpose(1, 0, 2), C_ssm.transpose(1, 0, 2), u.transpose(1, 0, 2))
            _, y = jax.lax.scan(step, h0, xs)
            y = y.transpose(1, 0, 2) + u * Dp
            y = y * jax.nn.silu(z)
            return jnp.einsum('bld,ed->ble', y, W_out)
        key = jax.random.key(seed)
        ks = jax.random.split(key, 16)
        s = lambda fan_in: 1.0 / np.sqrt(fan_in)
        inp = {'x': jax.random.normal(ks[0], (B, L, D_INPUT), jnp.float32), 'W_fc1': jax.random.normal(ks[1], (D_MODEL, D_INPUT), jnp.float32) * s(D_INPUT), 'b_fc1': jnp.zeros((D_MODEL,), jnp.float32), 'W_in': jax.random.normal(ks[2], (2 * D_INNER, D_MODEL), jnp.float32) * s(D_MODEL), 'conv_w': jax.random.normal(ks[3], (D_INNER, D_CONV), jnp.float32) * s(D_CONV), 'conv_b': jnp.zeros((D_INNER,), jnp.float32), 'W_xproj': jax.random.normal(ks[4], (DT_RANK + 2 * D_STATE, D_INNER), jnp.float32) * s(D_INNER), 'W_dt': jax.random.normal(ks[5], (D_INNER, DT_RANK), jnp.float32) * s(DT_RANK), 'b_dt': jax.random.uniform(ks[6], (D_INNER,), jnp.float32, -4.0, -2.0), 'A_log': jnp.log(jnp.broadcast_to(jnp.arange(1, D_STATE + 1, dtype=jnp.float32), (D_INNER, D_STATE))), 'D': jnp.ones((D_INNER,), jnp.float32), 'W_out': jax.random.normal(ks[7], (D_MODEL, D_INNER), jnp.float32) * s(D_INNER), 'W_fc2': jax.random.normal(ks[8], (D_OUTPUT, D_MODEL), jnp.float32) * s(D_MODEL), 'b_fc2': jnp.zeros((D_OUTPUT,), jnp.float32)}
        return inp
    _L0_ffn_all = _L0_ffn_setup()
    _L0_ffn_in = {k: v for k, v in _L0_ffn_all.items() if k in ('W_fc1', 'b_fc1', 'W_in', 'conv_w', 'conv_b', 'W_xproj', 'W_dt', 'b_dt', 'A_log', 'D', 'W_out', 'W_fc2', 'b_fc2')}
    del _L0_ffn_all
    return {'x': x, 'adj': adj, 'L0_gnn_weight': _L0_gnn_in['weight'], 'L0_gnn_bias': _L0_gnn_in['bias'], 'L0_ffn_W_fc1': _L0_ffn_in['W_fc1'], 'L0_ffn_b_fc1': _L0_ffn_in['b_fc1'], 'L0_ffn_W_in': _L0_ffn_in['W_in'], 'L0_ffn_conv_w': _L0_ffn_in['conv_w'], 'L0_ffn_conv_b': _L0_ffn_in['conv_b'], 'L0_ffn_W_xproj': _L0_ffn_in['W_xproj'], 'L0_ffn_W_dt': _L0_ffn_in['W_dt'], 'L0_ffn_b_dt': _L0_ffn_in['b_dt'], 'L0_ffn_A_log': _L0_ffn_in['A_log'], 'L0_ffn_D': _L0_ffn_in['D'], 'L0_ffn_W_out': _L0_ffn_in['W_out'], 'L0_ffn_W_fc2': _L0_ffn_in['W_fc2'], 'L0_ffn_b_fc2': _L0_ffn_in['b_fc2']}

def reference(x, adj, L0_gnn_weight, L0_gnn_bias, L0_ffn_W_fc1, L0_ffn_b_fc1, L0_ffn_W_in, L0_ffn_conv_w, L0_ffn_conv_b, L0_ffn_W_xproj, L0_ffn_W_dt, L0_ffn_b_dt, L0_ffn_A_log, L0_ffn_D, L0_ffn_W_out, L0_ffn_W_fc2, L0_ffn_b_fc2):
    import jax
    import jax.numpy as jnp

    def _L0_gnn_ref(inp, adj, weight, bias):
        import jax, jax.numpy as jnp
        import numpy as np
        N = 4096
        F_IN = 256
        F_OUT = 256
        support = jnp.matmul(inp, weight)
        return jnp.matmul(adj, support) + bias

    def _L0_ffn_ref(x, W_fc1, b_fc1, W_in, conv_w, conv_b, W_xproj, W_dt, b_dt, A_log, D, W_out, W_fc2, b_fc2):
        import jax, jax.numpy as jnp
        import numpy as np
        D_MODEL, D_STATE, D_CONV, D_INPUT, D_OUTPUT = (512, 16, 4, 256, 256)
        EXPAND = 2
        D_INNER = EXPAND * D_MODEL
        DT_RANK = (D_MODEL + 15) // 16
        B, L = (4, 1024)

        def _mamba(x, W_in, conv_w, conv_b, W_xproj, W_dt, b_dt, A_log, Dp, W_out):
            xz = jnp.einsum('bld,ed->ble', x, W_in)
            u, z = jnp.split(xz, 2, axis=-1)
            u_pad = jnp.pad(u, ((0, 0), (D_CONV - 1, 0), (0, 0)))
            u = sum((u_pad[:, k:k + u.shape[1], :] * conv_w[:, k] for k in range(D_CONV))) + conv_b
            u = jax.nn.silu(u)
            dbc = jnp.einsum('bld,ed->ble', u, W_xproj)
            dt, B_ssm, C_ssm = jnp.split(dbc, [DT_RANK, DT_RANK + D_STATE], axis=-1)
            delta = jax.nn.softplus(jnp.einsum('blr,dr->bld', dt, W_dt) + b_dt)
            A = -jnp.exp(A_log)

            def step(h, ins):
                d_t, B_t, C_t, u_t = ins
                dA = jnp.exp(d_t[..., None] * A)
                h = dA * h + (d_t * u_t)[..., None] * B_t[:, None, :]
                y_t = jnp.einsum('bds,bs->bd', h, C_t)
                return (h, y_t)
            h0 = jnp.zeros((u.shape[0], D_INNER, D_STATE), u.dtype)
            xs = (delta.transpose(1, 0, 2), B_ssm.transpose(1, 0, 2), C_ssm.transpose(1, 0, 2), u.transpose(1, 0, 2))
            _, y = jax.lax.scan(step, h0, xs)
            y = y.transpose(1, 0, 2) + u * Dp
            y = y * jax.nn.silu(z)
            return jnp.einsum('bld,ed->ble', y, W_out)
        h = jnp.einsum('bli,oi->blo', x, W_fc1) + b_fc1
        h = _mamba(h, W_in, conv_w, conv_b, W_xproj, W_dt, b_dt, A_log, D, W_out)
        return jnp.einsum('bld,od->blo', h, W_fc2) + b_fc2
    x = x + _L0_gnn_ref(_layernorm(x, axis=-1), adj, L0_gnn_weight, L0_gnn_bias)
    x = x + _L0_ffn_ref(_layernorm(x, axis=-1)[None], L0_ffn_W_fc1, L0_ffn_b_fc1, L0_ffn_W_in, L0_ffn_conv_w, L0_ffn_conv_b, L0_ffn_W_xproj, L0_ffn_W_dt, L0_ffn_b_dt, L0_ffn_A_log, L0_ffn_D, L0_ffn_W_out, L0_ffn_W_fc2, L0_ffn_b_fc2)[0]
    return x

_drawn_inputs = setup_inputs


def setup_inputs(seed=0):
    import zlib

    import numpy as np

    out = dict(_drawn_inputs(seed))
    spreads = {'L0_ffn_b_fc1': (0.0, 0.28),
     'L0_ffn_conv_b': (0.0, 0.383),
     'L0_ffn_D': (1.0, 0.2),
     'L0_ffn_b_fc2': (0.0, 0.1)}
    factors = {'L0_gnn_bias': 2.839, 'L0_ffn_W_dt': 10.559, 'L0_ffn_b_dt': 10.686}
    for name, (base, spread) in spreads.items():
        noise = np.random.default_rng([zlib.crc32(name.encode()), seed]).standard_normal(out[name].shape)
        drawn = base * np.exp(spread * noise) if base else spread * noise
        out[name] = jnp.asarray(drawn.astype(out[name].dtype))
    for name, factor in factors.items():
        out[name] = (out[name] * factor).astype(out[name].dtype)
    return out
```

```python
from contextlib import ExitStack

import concourse.bass as bass
from concourse import mybir

P = 128
F32 = mybir.dt.float32
BF16 = mybir.dt.bfloat16
ALU = mybir.AluOpType
ACT = mybir.ActivationFunctionType
EPS = 1e-5

T = 256
SUP = 2 * T
KG = 4
KL = 2
RING = 4
F = 256
FH = F // P
DM = 512
DMT = DM // P
DI = 1024
E = DI // P
NS = 16
R = 32
TAPS = 4
HIST = TAPS - 1
PAIRS = NS // 2
SLOTS = E * PAIRS

C_CONVW = 0
C_CONVB = C_CONVW + E * TAPS
C_D = C_CONVB + E
C_BDT = C_D + E
C_GB = C_BDT + E
C_B2 = C_GB + FH
C_B1 = C_B2 + FH
C_ALOG = C_B1 + DMT
C_ALL = C_ALOG + E * NS

G_MEAN, G_VAR, G_U, G_Z = 0, 1, 2, 2 + E // 2
G_XP = G_Z + E // 2
G_DT = G_XP + 1
G_BC = G_DT + E // 2
NP_ = G_BC + 2 * PAIRS

AT_OUT = 3
AT_STORE = 8
AT_MEAN = 9
AT_GREAD = 11
AT_G = 12
AT_VAR = 12
AT_RSTD = 13
AT_XN = 14
AT_U = 16
AT_Z = 24
AT_SILU = 32
AT_XP = 33
AT_XD = 38
AT_SPLIT = 39
AT_DT = 40
AT_BC = 57


def count(s, h, per, n):
    return s * (2 * per) + (h * per + n)


def gnn_share(h, i, total):
    slots = 2 * SLOTS - AT_G
    at = h * SLOTS + i - AT_G
    if at < 0:
        return 0, 0
    return at * total // slots, (at + 1) * total // slots


def graph_mamba_program(nc, adj_g, x_tok, x_fm, gnn_w, w_fc1, w_in_t, w_out, w_fc2_t, w_xp_t, w_dt_t,
                        columns, ident_in, pick_in, behind_in, support, out):
    n_sup = adj_g.shape[0]
    n_ld = adj_g.shape[1]
    n_grp = x_tok.shape[0]
    n_mm = n_ld * KL * FH
    assert n_sup >= 4 and n_ld % RING == 0 and n_ld > 2 * RING and n_grp % 2 == 0 and n_ld * KL == n_grp * KG

    with ExitStack() as ctx:
        def sb(name, shape, dt=F32):
            return ctx.enter_context(nc.sbuf_tensor(name, shape, dt))

        def bank(name):
            return ctx.enter_context(nc.psum_tensor(name, [P, 512], F32))

        def sem(name):
            return ctx.enter_context(nc.semaphore(name))

        adj_sb = sb("adj_sb", [P, RING, KL * SUP])
        sup_sb = sb("sup_sb", [P, RING, KL * F])
        bc = sb("bc", [P, 2, PAIRS, 2 * T])
        x1n = sb("x1n", [P, FH, SUP])
        xin = sb("xin", [P, FH, SUP])
        hold = sb("hold", [P, 2, FH, T])
        xc = sb("xc", [P, FH, T])
        sq = sb("sq", [P, FH, T])
        rstd = sb("rstd", [P, T])
        u = sb("u", [P, 2, E, T])
        z = sb("z", [P, 2, E, T])
        delta = sb("delta", [P, 2, E, T])
        du = sb("du", [P, 2, E, T])
        uraw = sb("uraw", [P, E, HIST + T])
        y2 = sb("y2", [P, E, T])
        ytmp = sb("ytmp", [P, T])
        xd = sb("xd", [P, T])
        xr1 = sb("xr1", [P, T])
        xr2 = sb("xr2", [P, T])
        xs = sb("xs", [P, T], BF16)
        spa = sb("spa", [P, 2 * T])
        spw = sb("spw", [P, 2 * T])
        spl = sb("spl", [P, 2 * T])
        bx = sb("bx", [P, 4, 2 * T])
        pr = sb("pr", [P, 4, 2 * T])
        state = sb("state", [P, E, NS])
        wc = sb("wc", [P, FH, 2 * DI])
        wo = sb("wo", [P, E, F])
        wxp = sb("wxp", [P, E, P])
        wdt = sb("wdt", [P, DI])
        cols = sb("cols", [P, C_ALL])
        a_neg = sb("a_neg", [P, E * NS])
        bcin = sb("bcin", [P, 2 * E])
        ident = sb("ident", [P, P])
        ones = sb("ones", [P, P])
        pick = sb("pick", [96, R], BF16)
        behind = sb("behind", [P, 2])
        eps = sb("eps", [P, 1])
        one = sb("one", [P, 1])
        ob = sb("ob", [P, FH, T])
        stats = sb("stats", [P, 2, KG, 6])
        mv = sb("mv", [P, 2, KG, 2])
        spare = sb("spare", [P, 1])
        rtok = sb("rtok", [P, 2, KG])
        win = bc[:, :, :, :].rearrange("p a b t -> p (a b t)").rearrange("p (k e) -> p k e", k=DMT)
        wout = du[:, :, :, :].rearrange("p a b t -> p (a b t)").rearrange("p (k e) -> p k e", k=DMT)
        wg = pr[:, 0, :].rearrange("p (f o) -> p f o", f=FH)
        wf1 = z[:, 0, 0:4, :]
        wf2 = z[:, 0, 4:8, :]
        xtok = [delta[:, t, 0:4, :] for t in range(2)]
        xnt = [u[:, t, :, :].rearrange("p e t -> p (e t)")[:, 0:FH * SUP].rearrange("p (f t) -> p f t", f=FH)
               for t in range(2)]
        sout = [y2[:, 4 * t:4 * t + 4, :] for t in range(2)]

        g_bank = [bank("g0"), bank("g1")]
        e_bank = [bank("e0"), bank("e1")]
        h_bank = [bank("h0"), bank("h1")]
        y_bank = bank("yb")
        m_bank = bank("mb")

        w_small = sem("w_small")
        w_big = sem("w_big")
        consts_set = sem("consts_set")
        a_set = sem("a_set")
        x_landed = [sem("x_landed0"), sem("x_landed1")]
        s_stats = sem("s_stats")
        s_var = sem("s_var")
        s_rstd = sem("s_rstd")
        s_xn = sem("s_xn")
        s_tr = sem("s_tr")
        s_trc = sem("s_trc")
        s_mm = sem("s_mm")
        s_out = sem("s_out")
        s_stored = [sem("s_stored0"), sem("s_stored1")]
        fold_mm = sem("fold_mm")
        fold_out = sem("fold_out")
        adj_landed = [sem(f"adj_landed{i}") for i in range(RING)]
        adj_used = sem("adj_used")
        xin_landed = sem("xin_landed")
        g_read = sem("g_read")
        p_mm = sem("p_mm")
        bc_done = sem("bc_done")
        ln_xc = sem("ln_xc")
        ln_sq = sem("ln_sq")
        ln_log = sem("ln_log")
        ln_rstd = sem("ln_rstd")
        ln_xn = sem("ln_xn")
        held = sem("held")
        u_raw = sem("u_raw")
        u_tap = sem("u_tap")
        u_conv = sem("u_conv")
        u_hist = sem("u_hist")
        z_raw = sem("z_raw")
        silu_done = sem("silu_done")
        xd_read = sem("xd_read")
        split = sem("split")
        sp_act = sem("sp_act")
        sp_dve = sem("sp_dve")
        sp_pool = sem("sp_pool")
        exp_done = sem("exp_done")
        bx_done = sem("bx_done")
        scan_done = sem("scan_done")
        pr_done = sem("pr_done")
        st_done = sem("st_done")
        st_zero = sem("st_zero")
        sum_done = sem("sum_done")
        y_free = sem("y_free")
        y_done = sem("y_done")
        o_mm = sem("o_mm")
        o_free = sem("o_free")
        o_stored = sem("o_stored")

        SP_SMALL, SP_BIG = 9 * 16, 4 * 16
        SPLITS = 7
        FOLDS = FH * 4 + E // 2 + 1

        block = ctx.enter_context(nc.Block())

        @block.sync
        def _(sp):
            def load_x(q, t, wait):
                if wait is not None:
                    sp.wait_ge(s_tr, wait)
                sp.dma_start(xtok[t].rearrange("p a b -> p (a b)"), x_tok[q]).then_inc(x_landed[t], 16)

            def store_s(q, t):
                sp.wait_ge(s_out, q * 2 + 2)
                sp.dma_start(support[q], sout[t].rearrange("p a b -> p (a b)")).then_inc(s_stored[t], 16)

            load_x(0, 0, None)
            sp.dma_start(cols[:, :], columns).then_inc(w_small, 16)
            sp.dma_start(ident[:, :], ident_in).then_inc(w_small, 16)
            sp.dma_start(wg[:, :, :], gnn_w).then_inc(w_small, 16)
            load_x(1, 1, None)
            sp.dma_start(pick[:, :], pick_in).then_inc(w_small, 16)
            sp.dma_start(behind[:, :], behind_in).then_inc(w_small, 16)
            sp.dma_start(wxp[:, :, :], w_xp_t).then_inc(w_small, 16)
            sp.dma_start(wdt[P - R:P, :], w_dt_t).then_inc(w_small, 16)
            sp.dma_start(wf1, w_fc1).then_inc(w_small, 16)
            sp.dma_start(wf2, w_fc2_t).then_inc(w_small, 16)
            for k in range(DMT // 2):
                sp.dma_start(win[:, 2 * k:2 * k + 2, :], w_in_t[:, 2 * k:2 * k + 2, :]).then_inc(w_big, 16)
                sp.dma_start(wout[:, 2 * k:2 * k + 2, :], w_out[:, 2 * k:2 * k + 2, :]).then_inc(w_big, 16)
            with sp.Fori(0, n_grp // 2 - 1) as j:
                for t in range(2):
                    load_x(j * 2 + (2 + t), t, j * 2 + (1 + t))
                    store_s(j * 2 + t, t)
            for t in range(2):
                store_s(n_grp - 2 + t, t)

            def load_adj(s, r):
                if not (isinstance(s, int) and s * n_ld + r < RING):
                    sp.wait_ge(adj_used, s * n_ld + (r - RING + 1))
                sp.dma_start(adj_sb[:, r % RING, :], adj_g[s, r]).then_inc(adj_landed[r % RING], 16)
                if isinstance(s, int) and s == 0 and r < RING:
                    for t in range(2):
                        sp.wait_ge(s_stored[t], 8 * n_grp)
                sp.dma_start(sup_sb[:, r % RING, :], support[r * KL // KG][:, r * KL % KG * F:(r * KL % KG + KL) * F]).then_inc(adj_landed[r % RING], 16)

            def load_xin(s, wait):
                if wait:
                    sp.wait_ge(g_read, s * FH)
                sp.dma_start(xin[:, :, :], x_fm[s]).then_inc(xin_landed, 16)

            def store_out(s, h):
                sp.wait_ge(o_free, count(s, h, FH, FH))
                sp.dma_start(out[s * 2 + h], ob[:, :, :]).then_inc(o_stored, 16)

            def iteration(s, first=False, adj=True):
                for r in range(n_ld):
                    if adj and r < RING:
                        load_adj(s + 2, r)
                if not first:
                    store_out(s - 1, 1)
                for r in range(RING, n_ld):
                    if adj and r < 3 * n_ld // 4:
                        load_adj(s + 2, r)
                    if adj and r == RING + 1:
                        load_xin(s + 2, True)
                store_out(s, 0)
                for r in range(3 * n_ld // 4, n_ld):
                    if adj and r >= RING:
                        load_adj(s + 2, r)

            load_xin(0, False)
            for r in range(n_ld):
                load_adj(0, r)
            for r in range(n_ld):
                load_adj(1, r)
                if r == RING + 1:
                    load_xin(1, True)
            iteration(0, first=True)
            with sp.Fori(1, n_sup - 2) as s:
                iteration(s)
            iteration(n_sup - 2, adj=False)
            iteration(n_sup - 1, adj=False)
            store_out(n_sup - 1, 1)
            sp.wait_ge(o_stored, 16 * 2 * n_sup)

        @block.gpsimd
        def _(pool):
            pool.memset(eps[:, :], EPS).then_inc(consts_set, 1)
            pool.memset(one[:, :], 1.0).then_inc(consts_set, 1)
            pool.memset(ones[:, :], 1.0 / F).then_inc(consts_set, 1)
            pool.memset(state[:, :, :], 0.0).then_inc(st_zero, 1)
            pool.memset(uraw[:, :, 0:HIST], 0.0).then_inc(st_zero, 1)

            pool.wait_ge(consts_set, 3)
            pool.wait_ge(w_small, SP_SMALL)

            def copy(dst, src):
                n, m = src.shape[0], src.shape[-1]
                lo = src.start_partition()
                by = one[lo:lo + n, :]
                by = by.to_broadcast([n, m]) if len(src.shape) == 2 else by.unsqueeze(1).to_broadcast(list(src.shape))
                return pool.tensor_tensor(dst, src, by, ALU.mult)

            def unit(s, h, i):
                d, np_ = divmod(i, PAIRS)
                if i == 0:
                    pool.wait_ge(sp_pool, count(s, h, E, E))
                if d == 0:
                    pool.wait_ge(bc_done, count(s, h, 2 * PAIRS, 2 * np_ + 1))
                if not (isinstance(s, int) and count(s, h, SLOTS, i) < 4):
                    pool.wait_ge(scan_done, count(s, h, 2 * SLOTS, 2 * (i - 3)))
                v = du[:, h, d, :].unsqueeze(1).to_broadcast([P, 2, T])
                pool.tensor_tensor(bx[:, i % 4, :].rearrange("p (a t) -> p a t", a=2), v,
                                   bc[:, 0, np_, :].rearrange("p (a t) -> p a t", a=2),
                                   ALU.mult).then_inc(bx_done, 1)

            def pieces(s, h, i):
                if i == AT_U + 8:
                    pool.wait_ge(u_conv, count(s, h, 3 * E, 3 * E))
                    tail, head = uraw[:, :, T:T + HIST], uraw[:, :, 0:HIST]
                    copy(head, tail).then_inc(u_hist, 1)
                if i == AT_SPLIT:
                    pool.wait_ge(xd_read, count(s, h, 1, 1))
                    copy(xs[:, :], xd[:, :]).then_inc(split, 1)
                    for n, (was, rest) in enumerate(((xd, xr1), (xr1, xr2))):
                        pool.wait_ge(split, count(s, h, SPLITS, 3 * n + 1))
                        by = behind[:, n:n + 1].to_broadcast([P, T])
                        pool.tensor_tensor(rest[:, :], xs[:, :], by, ALU.mult).then_inc(split, 1)
                        pool.wait_ge(split, count(s, h, SPLITS, 3 * n + 2))
                        pool.tensor_tensor(rest[:, :], was[:, :], rest[:, :], ALU.subtract).then_inc(split, 1)
                        pool.wait_ge(split, count(s, h, SPLITS, 3 * n + 3))
                        copy(xs[:, :], rest[:, :]).then_inc(split, 1)
                if i >= AT_DT + 3 and (i - AT_DT - 3) % 2 == 0 and (i - AT_DT - 3) // 2 < E // 2:
                    b = (i - AT_DT - 3) // 2
                    pool.wait_ge(sp_dve, count(s, h, E, 2 * b + 2))
                    pool.wait_ge(sp_act, count(s, h, 3 * E, 6 * b + 6))
                    dl = delta[:, h, 2 * b:2 * b + 2, :].rearrange("p a t -> p (a t)")
                    pool.tensor_tensor(dl, dl, spl[:, :], ALU.add).then_inc(sp_pool, 1)
                    pool.wait_ge(sp_pool, count(s, h, E, 2 * b + 1))
                    pool.tensor_tensor(du[:, h, 2 * b:2 * b + 2, :].rearrange("p a t -> p (a t)"), dl,
                                       u[:, h, 2 * b:2 * b + 2, :].rearrange("p a t -> p (a t)"),
                                       ALU.mult).then_inc(sp_pool, 1)

            def chunk(s, h, following=True):
                for i in range(SLOTS):
                    unit(s, h, i)
                    if following:
                        pieces(s + h, 1 - h, i)

            def iteration(s, following=True):
                chunk(s, 0)
                chunk(s, 1, following)

            for i in range(SLOTS):
                pieces(0, 0, i)
            iteration(0)
            with pool.Fori(1, n_sup - 2) as s:
                iteration(s)
            iteration(n_sup - 2)
            iteration(n_sup - 1, following=False)

        @block.scalar
        def _(act):
            act.preload_act_table_set("natural_log_exp_and_others")
            act.wait_ge(w_small, SP_SMALL)
            act.activation(a_neg[:, :], cols[:, C_ALOG:C_ALL], ACT.Exp).then_inc(a_set, 1)
            act.wait_ge(a_set, 1)
            act.activation(a_neg[:, :], a_neg[:, :], ACT.Identity, scale=-1.0).then_inc(a_set, 1)
            act.wait_ge(consts_set, 3)

            def rstd_tok(q, t):
                act.wait_ge(s_var, q + 1)
                act.activation(rtok[:, t, :], mv[:, t, :, 1], ACT.Ln, bias=eps[:, :]).then_inc(s_rstd, 1)
                act.wait_ge(s_rstd, q * 2 + 1)
                act.activation(rtok[:, t, :], rtok[:, t, :], ACT.Exp, scale=-0.5).then_inc(s_rstd, 1)

            def read_transposed(q, t, free):
                act.wait_ge(s_tr, q + 1)
                if free is not None:
                    act.wait_ge(s_mm, free)
                for f in range(FH):
                    act.activation(xnt[t][:, f, :], [e_bank, h_bank][t][f][:, :], ACT.Copy).then_inc(s_trc, 1)

            rstd_tok(0, 0)
            rstd_tok(1, 1)
            read_transposed(0, 0, None)
            rstd_tok(2, 0)
            read_transposed(1, 1, None)
            with act.Fori(1, n_grp // 2 - 1) as j:
                rstd_tok(j * 2 + 1, 1)
                read_transposed(j * 2, 0, j * 2 - 1)
                rstd_tok(j * 2 + 2, 0)
                read_transposed(j * 2 + 1, 1, j * 2)
            rstd_tok(n_grp - 1, 1)
            read_transposed(n_grp - 2, 0, n_grp - 3)
            read_transposed(n_grp - 1, 1, n_grp - 2)

            for n in range(FOLDS):
                src = [e_bank, h_bank][n // 2 % 2][n % 2]
                act.wait_ge(fold_mm, n + 1)
                if n < FH * 4:
                    act.activation(wc[:, n // 4, n % 4 * 512:n % 4 * 512 + 512], src[:, :], ACT.Copy).then_inc(fold_out, 1)
                elif n < FOLDS - 1:
                    d = 2 * (n - FH * 4)
                    act.activation(wo[:, d:d + 2, :].rearrange("p a t -> p (a t)"), src[:, :], ACT.Copy).then_inc(fold_out, 1)
                else:
                    act.activation(bcin[:, :], src[:, 0:2 * E], ACT.Copy).then_inc(fold_out, 1)

            def exps(s, h, i):
                d, np_ = divmod(i, PAIRS)
                if i == 0:
                    act.wait_ge(sp_pool, count(s, h, E, E))
                if not (isinstance(s, int) and count(s, h, SLOTS, i) < 2):
                    act.wait_ge(scan_done, count(s, h, 2 * SLOTS, 2 * (i - 1)))
                for a in range(2):
                    n = d * NS + 2 * np_ + a
                    ins = act.activation(e_bank[i % 2][:, a * T:(a + 1) * T], delta[:, h, d, :], ACT.Exp,
                                         scale=a_neg[:, n:n + 1])
                ins.then_inc(exp_done, 1)

            def pieces(s, h, i):
                half = slice(h * T, h * T + T)
                if i == AT_MEAN:
                    if not (isinstance(s, int) and s == 0):
                        act.wait_ge(o_free, count(s - 1, h, FH, FH))
                    act.wait_ge(g_read, s * FH + FH)
                    act.activation(hold[:, h, :, :], x1n[:, :, half], ACT.Copy).then_inc(held, 1)
                if i == AT_MEAN + 2:
                    act.wait_ge(ln_xc, count(s, h, 1, 1))
                    act.activation(sq[:, :, :], xc[:, :, :], ACT.Square).then_inc(ln_sq, 1)
                if i == AT_RSTD:
                    act.wait_ge(p_mm, count(s, h, NP_, G_VAR + 1))
                    act.activation(rstd[:, :], m_bank[:, 0:T], ACT.Ln, bias=eps[:, :]).then_inc(ln_log, 1)
                    act.wait_ge(ln_log, count(s, h, 1, 1))
                    act.activation(rstd[:, :], rstd[:, :], ACT.Exp, scale=-0.5).then_inc(ln_rstd, 1)
                for g in range(E // 2):
                    if i == AT_U + 2 * g + 1:
                        act.wait_ge(p_mm, count(s, h, NP_, G_U + g + 1))
                        if g == 0 and isinstance(s, int) and s == 0 and h == 0:
                            act.wait_ge(st_zero, 2)
                        elif g == 0:
                            act.wait_ge(u_hist, count(s, h, 1, 0))
                        for a in range(2):
                            e = 2 * g + a
                            act.activation(uraw[:, e, HIST:HIST + T], m_bank[:, a * T:(a + 1) * T], ACT.Identity,
                                           bias=bcin[:, e:e + 1]).then_inc(u_raw, 1)
                        act.wait_ge(u_raw, count(s, h, E, 2 * g + 2))
                        for a in range(2):
                            e = 2 * g + a
                            ins = act.activation(u[:, h, e, :], uraw[:, e, 0:T], ACT.Identity,
                                                 scale=cols[:, C_CONVW + e * TAPS:C_CONVW + e * TAPS + 1],
                                                 bias=cols[:, C_CONVB + e:C_CONVB + e + 1])
                            ins.then_inc(u_tap, 1)
                    if i == AT_Z + 2 * g + 1:
                        act.wait_ge(p_mm, count(s, h, NP_, G_Z + g + 1))
                        for a in range(2):
                            e = 2 * g + a
                            act.activation(z[:, h, e, :], m_bank[:, a * T:(a + 1) * T], ACT.Identity,
                                           bias=bcin[:, E + e:E + e + 1]).then_inc(z_raw, 1)
                    if i == AT_DT + 2 * g + 1:
                        c = count(s, h, 3 * E, 6 * g)
                        act.wait_ge(p_mm, count(s, h, NP_, G_DT + g + 1))
                        for a in range(2):
                            e = 2 * g + a
                            act.activation(delta[:, h, e, :], m_bank[:, a * T:(a + 1) * T], ACT.Identity,
                                           bias=cols[:, C_BDT + e:C_BDT + e + 1]).then_inc(sp_act, 1)
                        act.wait_ge(sp_act, c + 2)
                        if not (isinstance(s, int) and s == 0 and h == 0 and g == 0):
                            act.wait_ge(sp_pool, count(s, h, E, 2 * g - 1))
                        x2 = delta[:, h, 2 * g:2 * g + 2, :].rearrange("p a t -> p (a t)")
                        act.activation(spa[:, :], x2, ACT.Abs).then_inc(sp_act, 1)
                        act.wait_ge(sp_act, c + 3)
                        act.activation(spa[:, :], spa[:, :], ACT.Exp, scale=-1.0).then_inc(sp_act, 1)
                        act.wait_ge(sp_act, c + 4)
                        act.activation(spw[:, :], spa[:, :], ACT.Identity, bias=1.0).then_inc(sp_act, 1)
                        act.activation(spl[:, :], spa[:, :], ACT.Ln, bias=1.0).then_inc(sp_act, 1)
                if i == AT_SILU:
                    act.wait_ge(u_conv, count(s, h, 3 * E, 3 * E))
                    act.wait_ge(z_raw, count(s, h, E, E))
                    uu = u[:, h, :, :].rearrange("p a t -> p (a t)")
                    zz = z[:, h, :, :].rearrange("p a t -> p (a t)")
                    act.activation(uu, uu, ACT.Silu).then_inc(silu_done, 1)
                    act.activation(zz, zz, ACT.Silu).then_inc(silu_done, 1)
                    act.preload_act_table_set("natural_log_exp_and_others")
                for np_ in range(PAIRS):
                    if i == min(AT_BC + np_, SLOTS - 1):
                        for w in range(2):
                            if not (isinstance(s, int) and s == 0 and h == 0):
                                act.wait_ge([bx_done, pr_done][w], count(s, h, SLOTS, SLOTS - PAIRS - SLOTS + np_ + 1))
                            act.wait_ge(p_mm, count(s, h, NP_, G_BC + 2 * np_ + w + 1))
                            act.activation(bc[:, w, np_, :], m_bank[:, :], ACT.Copy).then_inc(bc_done, 1)

            def chunk(s, h, following=True):
                for i in range(SLOTS):
                    if i + 1 < SLOTS:
                        exps(s, h, i + 1)
                    elif following:
                        exps(s + h, 1 - h, 0)
                    if following:
                        pieces(s + h, 1 - h, i)

            def iteration(s, following=True):
                chunk(s, 0)
                chunk(s, 1, following)

            for i in range(SLOTS):
                pieces(0, 0, i)
            exps(0, 0, 0)
            iteration(0)
            with act.Fori(1, n_sup - 2) as s:
                iteration(s)
            iteration(n_sup - 2)
            iteration(n_sup - 1, following=False)

        @block.vector
        def _(dve):
            def stats_tok(q, t, landed):
                dve.wait_ge(x_landed[t], landed)
                for kt in range(KG):
                    dve.bn_stats(stats[:, t, kt, :], xtok[t][:, kt, :]).then_inc(s_stats, 1)
                dve.wait_ge(s_stats, q * KG + KG)
                dve.memset(spare[:, :], 0.0)
                for kt in range(KG):
                    ins = dve.bn_aggr(mv[:, t, kt, :], stats[:, t, kt, :])
                ins.then_inc(s_var, 1)

            def apply_tok(q, t):
                dve.wait_ge(s_rstd, q * 2 + 2)
                for kt in range(KG):
                    dve.tensor_scalar(xtok[t][:, kt, :], xtok[t][:, kt, :], mv[:, t, kt, 0:1], rtok[:, t, kt:kt + 1],
                                      ALU.subtract, ALU.mult).then_inc(s_xn, 1)

            def read_support(q, t, stored):
                dve.wait_ge(s_mm, q + 1)
                if stored is not None:
                    dve.wait_ge(s_stored[t], stored)
                for b in range(2):
                    src = [g_bank, [y_bank, m_bank]][t][b]
                    dve.tensor_copy(sout[t].rearrange("p a f -> p (a f)")[:, b * 512:b * 512 + 512],
                                    src[:, :]).then_inc(s_out, 1)

            stats_tok(0, 0, 16)
            apply_tok(0, 0)
            stats_tok(1, 1, 16)
            apply_tok(1, 1)
            read_support(0, 0, None)
            stats_tok(2, 0, 32)
            apply_tok(2, 0)
            read_support(1, 1, None)
            with dve.Fori(1, n_grp // 2 - 1) as j:
                stats_tok(j * 2 + 1, 1, j * 16 + 16)
                apply_tok(j * 2 + 1, 1)
                read_support(j * 2, 0, j * 16)
                stats_tok(j * 2 + 2, 0, j * 16 + 32)
                apply_tok(j * 2 + 2, 0)
                read_support(j * 2 + 1, 1, j * 16)
            stats_tok(n_grp - 1, 1, n_grp // 2 * 16)
            apply_tok(n_grp - 1, 1)
            read_support(n_grp - 2, 0, 8 * (n_grp - 2))
            read_support(n_grp - 1, 1, 8 * (n_grp - 2))

            dve.wait_ge(w_small, SP_SMALL)
            dve.wait_ge(st_zero, 2)

            def read_gnn(s):
                dve.wait_ge(adj_used, s * n_ld + n_ld)
                dve.wait_ge(xin_landed, s * 16 + 16)
                if not (isinstance(s, int) and s == 0):
                    dve.wait_ge(held, s * 2)
                    dve.wait_ge(ln_xc, s * 2)
                for f in range(FH):
                    dve.scalar_tensor_tensor(x1n[:, f, :], g_bank[f][:, :], cols[:, C_GB + f:C_GB + f + 1],
                                             xin[:, f, :], ALU.add, ALU.add).then_inc(g_read, 1)

            def unit_scan(s, h, i):
                d, np_ = divmod(i, PAIRS)
                dve.wait_ge(exp_done, count(s, h, SLOTS, i + 1))
                dve.wait_ge(bx_done, count(s, h, SLOTS, i + 1))
                first = isinstance(s, int) and s == 0 and h == 0
                if not (first and i < 2):
                    dve.wait_ge(pr_done, count(s, h, SLOTS, i - 1))
                    dve.wait_ge(st_done, count(s, h, SLOTS, i - 1))
                for a in range(2):
                    n = 2 * np_ + a
                    dve.tensor_tensor_scan(h_bank[i % 2][:, a * T:(a + 1) * T], e_bank[i % 2][:, a * T:(a + 1) * T],
                                           bx[:, i % 4, a * T:(a + 1) * T], state[:, d, n:n + 1],
                                           ALU.mult, ALU.add).then_inc(scan_done, 1)

            def unit_mult(s, h, i):
                d, np_ = divmod(i, PAIRS)
                dve.wait_ge(scan_done, count(s, h, 2 * SLOTS, 2 * i + 2))
                if d == 0:
                    dve.wait_ge(bc_done, count(s, h, 2 * PAIRS, 2 * np_ + 2))
                if not (isinstance(s, int) and count(s, h, SLOTS, i) < 4):
                    dve.wait_ge(sum_done, count(s, h, SLOTS, i - 3))
                dve.tensor_tensor(pr[:, i % 4, :], h_bank[i % 2][:, :], bc[:, 1, np_, :], ALU.mult).then_inc(pr_done, 1)
                last = h_bank[i % 2][:, :].rearrange("p (a t) -> p a t", a=2)[:, :, T - 1]
                dve.tensor_copy(state[:, d, 2 * np_:2 * np_ + 2], last).then_inc(st_done, 1)

            def gate(s, h, d):
                dve.wait_ge(sum_done, count(s, h, SLOTS, (d + 1) * PAIRS))
                if d == 0 and not (isinstance(s, int) and s == 0 and h == 0):
                    dve.wait_ge(o_mm, count(s, h, 1, 0))
                if not (isinstance(s, int) and s == 0 and h == 0 and d == 0):
                    dve.wait_ge(y_done, count(s, h, E, d))
                dve.scalar_tensor_tensor(ytmp[:, :], u[:, h, d, :], cols[:, C_D + d:C_D + d + 1], y_bank[:, 0:T],
                                         ALU.mult, ALU.add).then_inc(y_free, 1)
                dve.wait_ge(y_free, count(s, h, E, d + 1))
                dve.tensor_tensor(y2[:, d, :], ytmp[:, :], z[:, h, d, :], ALU.mult).then_inc(y_done, 1)

            def finish(s, h):
                dve.wait_ge(o_mm, count(s, h, 1, 1))
                if not (isinstance(s, int) and s == 0 and h == 0):
                    dve.wait_ge(o_stored, count(s, h, 16, 0))
                for f in range(FH):
                    dve.scalar_tensor_tensor(ob[:, f, :], m_bank[:, f * T:(f + 1) * T], cols[:, C_B2 + f:C_B2 + f + 1],
                                             hold[:, h, f, :], ALU.add, ALU.add).then_inc(o_free, 1)

            def pieces(s, h, i):
                half = slice(h * T, h * T + T)
                if i == AT_MEAN + 1:
                    dve.wait_ge(p_mm, count(s, h, NP_, G_MEAN + 1))
                    m = m_bank[:, 0:T].unsqueeze(1).to_broadcast([P, FH, T])
                    dve.tensor_tensor(xc[:, :, :], x1n[:, :, half], m, ALU.subtract).then_inc(ln_xc, 1)
                if i == AT_XN:
                    dve.wait_ge(ln_rstd, count(s, h, 1, 1))
                    r = rstd[:, :].unsqueeze(1).to_broadcast([P, FH, T])
                    dve.tensor_tensor(xc[:, :, :], xc[:, :, :], r, ALU.mult).then_inc(ln_xn, 1)
                for g in range(E // 2):
                    if i == AT_U + 2 * g + 2:
                        dve.wait_ge(u_tap, count(s, h, E, 2 * g + 2))
                        for j in range(1, TAPS):
                            if j > 1:
                                dve.wait_ge(u_conv, count(s, h, 3 * E, 6 * g + 2 * (j - 1)))
                            for e in (2 * g, 2 * g + 1):
                                w = C_CONVW + e * TAPS + j
                                dve.scalar_tensor_tensor(u[:, h, e, :], uraw[:, e, j:j + T], cols[:, w:w + 1],
                                                         u[:, h, e, :], ALU.mult, ALU.add).then_inc(u_conv, 1)
                    if i == AT_DT + 2 * g + 2:
                        dve.wait_ge(sp_act, count(s, h, 3 * E, 6 * g + 5))
                        dve.scalar_tensor_tensor(spw[:, :], spw[:, :], -1.0, spa[:, :], ALU.add,
                                                 ALU.subtract).then_inc(sp_dve, 1)
                        dve.wait_ge(sp_dve, count(s, h, E, 2 * g + 1))
                        x2 = delta[:, h, 2 * g:2 * g + 2, :].rearrange("p a t -> p (a t)")
                        dve.scalar_tensor_tensor(x2, x2, 0.0, spw[:, :], ALU.max,
                                                 ALU.subtract).then_inc(sp_dve, 1)
                if i == AT_XD:
                    dve.wait_ge(p_mm, count(s, h, NP_, G_XP + 1))
                    dve.tensor_copy(xd[:, :], m_bank[:, 0:T]).then_inc(xd_read, 1)

            def chunk(s, h, before=True, following=True, gnn=True):
                for i in range(SLOTS):
                    unit_scan(s, h, i)
                    if i > 0:
                        unit_mult(s, h, i - 1)
                    elif before:
                        unit_mult(s - 1 + h, 1 - h, SLOTS - 1)
                    if i % PAIRS == 2:
                        if i > PAIRS:
                            gate(s, h, i // PAIRS - 1)
                        elif before:
                            gate(s - 1 + h, 1 - h, E - 1)
                    if i == AT_STORE and before:
                        finish(s - 1 + h, 1 - h)
                    if i == AT_GREAD and h == 0 and gnn:
                        read_gnn(s + 1)
                    if following:
                        pieces(s + h, 1 - h, i)

            def iteration(s, before=True, following=True, gnn=True):
                chunk(s, 0, before=before, gnn=gnn)
                chunk(s, 1, following=following)

            read_gnn(0)
            for i in range(SLOTS):
                pieces(0, 0, i)
            iteration(0, before=False)
            with dve.Fori(1, n_sup - 2) as s:
                iteration(s)
            iteration(n_sup - 2)
            iteration(n_sup - 1, following=False, gnn=False)
            unit_mult(n_sup - 1, 1, SLOTS - 1)
            gate(n_sup - 1, 1, E - 1)
            finish(n_sup - 1, 1)

        @block.tensor
        def _(pe):
            pe.wait_ge(w_small, SP_SMALL)
            pe.wait_ge(consts_set, 3)

            def transposes(q, t, free):
                pe.wait_ge(s_xn, q * KG + KG)
                if free is not None:
                    pe.wait_ge(s_trc, free)
                for f in range(FH):
                    for kt in range(KG):
                        ins = pe.transpose([e_bank, h_bank][t][f][:, kt * P:(kt + 1) * P],
                                           xtok[t][:, kt, f * P:(f + 1) * P], ident[:, :])
                ins.then_inc(s_tr, 1)

            def products(q, t, free):
                pe.wait_ge(s_trc, q * 2 + 2)
                if free is not None:
                    pe.wait_ge(s_out, free)
                for kt in range(KG):
                    dst = [g_bank, [y_bank, m_bank]][t][kt // 2]
                    for f in range(FH):
                        ins = pe.matmul(dst[:, kt % 2 * F:kt % 2 * F + F], xnt[t][:, f, kt * P:(kt + 1) * P],
                                        wg[:, f, :], start=(f == 0), stop=(f == FH - 1))
                ins.then_inc(s_mm, 1)

            transposes(0, 0, None)
            transposes(1, 1, None)
            products(0, 0, None)
            transposes(2, 0, 2)
            products(1, 1, None)
            with pe.Fori(1, n_grp // 2 - 1) as j:
                transposes(j * 2 + 1, 1, j * 4)
                products(j * 2, 0, j * 4 - 2)
                transposes(j * 2 + 2, 0, j * 4 + 2)
                products(j * 2 + 1, 1, j * 4)
            transposes(n_grp - 1, 1, 2 * (n_grp - 2))
            products(n_grp - 2, 0, 2 * (n_grp - 3))
            products(n_grp - 1, 1, 2 * (n_grp - 2))

            pe.wait_ge(w_big, SP_BIG)
            for n in range(FOLDS):
                dst = [e_bank, h_bank][n // 2 % 2][n % 2]
                if n < 4:
                    pe.wait_ge(s_trc, 2 * n_grp)
                else:
                    pe.wait_ge(fold_out, n - 3)
                if n < FH * 4:
                    f, c = divmod(n, 4)
                    for k in range(DMT):
                        ins = pe.matmul(dst[:, :], wf1[:, k, f * P:(f + 1) * P], win[:, k, c * 512:(c + 1) * 512],
                                        start=(k == 0), stop=(k == DMT - 1))
                elif n < FOLDS - 1:
                    for a in range(2):
                        d = 2 * (n - FH * 4) + a
                        for k in range(DMT):
                            ins = pe.matmul(dst[:, a * F:(a + 1) * F], wout[:, k, d * P:(d + 1) * P], wf2[:, k, :],
                                            start=(k == 0), stop=(k == DMT - 1))
                else:
                    for e in range(2 * E):
                        for k in range(DMT):
                            ins = pe.matmul(dst[:, e:e + 1], win[:, k, e * P:(e + 1) * P],
                                            cols[:, C_B1 + k:C_B1 + k + 1], start=(k == 0), stop=(k == DMT - 1))
                ins.then_inc(fold_mm, 1)

            def gnn(s, lo, hi):
                for m in range(lo, hi):
                    kt, f = divmod(m, FH)
                    r = kt // KL
                    if m == 0:
                        if isinstance(s, int) and s == 0:
                            pe.wait_ge(s_out, 2 * n_grp)
                        else:
                            pe.wait_ge(g_read, s * FH)
                    if kt % KL == 0 and f == 0:
                        per = n_ld // RING * 32
                        pe.wait_ge(adj_landed[r % RING], s * per + 32 * (r // RING + 1))
                    ins = pe.matmul(g_bank[f][:, :],
                                    sup_sb[:, r % RING, kt % KL * F + f * P:kt % KL * F + (f + 1) * P],
                                    adj_sb[:, r % RING, kt % KL * SUP:(kt % KL + 1) * SUP],
                                    start=(kt == 0), stop=(kt == n_ld * KL - 1))
                    if kt % KL == KL - 1 and f == FH - 1:
                        ins.then_inc(adj_used, 1)

            def sums(s, h, i):
                d, np_ = divmod(i, PAIRS)
                first = isinstance(s, int) and s == 0 and h == 0
                pe.wait_ge(pr_done, count(s, h, SLOTS, i + 1))
                if np_ == 0 and not (first and d == 0):
                    pe.wait_ge(y_free, count(s, h, E, d))
                for a in range(2):
                    ins = pe.matmul(y_bank[:, 0:T], ident[:, :], pr[:, i % 4, a * T:(a + 1) * T],
                                    start=(np_ == 0 and a == 0), stop=(np_ == PAIRS - 1 and a == 1))
                ins.then_inc(sum_done, 1)

            def out_product(s, h, j, groups=2):
                if j == 0:
                    pe.wait_ge(y_done, count(s, h, E, E))
                    pe.wait_ge(bc_done, count(s, h, 2 * PAIRS, 2 * PAIRS * groups))
                for n in range(4 * j, 4 * j + 4):
                    f, d = divmod(n, E)
                    ins = pe.matmul(m_bank[:, f * T:(f + 1) * T], wo[:, d, f * P:(f + 1) * P], y2[:, d, :],
                                    start=(d == 0), stop=(d == E - 1))
                if j == 3:
                    ins.then_inc(o_mm, 1)

            def pieces(s, h, i, before):
                half = slice(h * T, h * T + T)

                if i == AT_MEAN:
                    if before:
                        pe.wait_ge(o_free, count(s - 1, h, FH, FH))
                    elif not (isinstance(s, int) and s == 0 and h == 0):
                        pe.wait_ge(bc_done, count(s, h, 2 * PAIRS, 0))
                    pe.wait_ge(g_read, s * FH + FH)
                    for f in range(FH):
                        ins = pe.matmul(m_bank[:, 0:T], ones[:, :], x1n[:, f, half], start=(f == 0), stop=(f == FH - 1))
                    ins.then_inc(p_mm, 1)
                if i == AT_VAR:
                    pe.wait_ge(ln_sq, count(s, h, 1, 1))
                    for f in range(FH):
                        ins = pe.matmul(m_bank[:, 0:T], ones[:, :], sq[:, f, :], start=(f == 0), stop=(f == FH - 1))
                    ins.then_inc(p_mm, 1)
                for g in range(E // 2):
                    for at, base, off in ((AT_U, G_U, 0), (AT_Z, G_Z, E)):
                        if i == at + 2 * g:
                            if off == 0 and g == 0:
                                pe.wait_ge(ln_xn, count(s, h, 1, 1))
                            elif off == 0:
                                pe.wait_ge(u_raw, count(s, h, E, 2 * g))
                            elif g == 0:
                                pe.wait_ge(u_raw, count(s, h, E, E))
                            else:
                                pe.wait_ge(z_raw, count(s, h, E, 2 * g))
                            for a in range(2):
                                e = off + 2 * g + a
                                for f in range(FH):
                                    ins = pe.matmul(m_bank[:, a * T:(a + 1) * T], wc[:, f, e * P:(e + 1) * P], xc[:, f, :],
                                                    start=(f == 0), stop=(f == FH - 1))
                            ins.then_inc(p_mm, 1)
                    if i == AT_DT + 2 * g:
                        if g == 0:
                            pe.wait_ge(xd_read, count(s, h, 1, 1))
                        else:
                            pe.wait_ge(sp_act, count(s, h, 3 * E, 6 * g - 4))
                        for a in range(2):
                            e = 2 * g + a
                            ins = pe.matmul(m_bank[:, a * T:(a + 1) * T], wdt[P - R:P, e * P:(e + 1) * P], xd[P - R:P, :],
                                            start=True, stop=True)
                        ins.then_inc(p_mm, 1)
                if AT_XP <= i < AT_XP + 4:
                    if i == AT_XP:
                        pe.wait_ge(z_raw, count(s, h, E, E))
                        pe.wait_ge(silu_done, count(s, h, 2, 1))
                    for e in (2 * (i - AT_XP), 2 * (i - AT_XP) + 1):
                        ins = pe.matmul(m_bank[:, 0:T], wxp[:, e, :], u[:, h, e, :], start=(e == 0), stop=(e == E - 1))
                    if i == AT_XP + 3:
                        ins.then_inc(p_mm, 1)
                for np_ in range(PAIRS):
                    if i == min(AT_BC + np_, SLOTS - 1):
                        for w in range(2):
                            if np_ == 0 and w == 0:
                                pe.wait_ge(split, count(s, h, SPLITS, SPLITS))
                                pe.wait_ge(sp_act, count(s, h, 3 * E, 3 * E - 4))
                            else:
                                pe.wait_ge(bc_done, count(s, h, 2 * PAIRS, 2 * np_ + w))
                            for a in range(2):
                                row = w * NS + 2 * np_ + a
                                ins = pe.matmul(m_bank[:, a * T:(a + 1) * T],
                                                pick[:, row:row + 1].to_broadcast([96, P]), xs[0:96, :],
                                                start=True, stop=True)
                            ins.then_inc(p_mm, 1)

            def chunk(s, h, before=True, following=True, product=True):
                for i in range(SLOTS):
                    if following:
                        pieces(s + h, 1 - h, i, before)
                    if before and AT_OUT <= i < AT_OUT + 4:
                        out_product(s - 1 + h, 1 - h, i - AT_OUT)
                    if product:
                        gnn(s + 2, *gnn_share(h, i, n_mm))
                    if i >= 2:
                        sums(s, h, i - 2)
                    elif before:
                        sums(s - 1 + h, 1 - h, SLOTS - 2 + i)

            def iteration(s, before=True, following=True, product=True):
                chunk(s, 0, before=before, product=product)
                chunk(s, 1, following=following, product=product)

            gnn(0, 0, n_mm)
            for i in range(SLOTS):
                pieces(0, 0, i, False)
                gnn(1, i * n_mm // SLOTS, (i + 1) * n_mm // SLOTS)
            iteration(0, before=False)
            with pe.Fori(1, n_sup - 2) as s:
                iteration(s)
            iteration(n_sup - 2, product=False)
            iteration(n_sup - 1, following=False, product=False)
            for i in range(2):
                sums(n_sup - 1, 1, SLOTS - 2 + i)
            for j in range(4):
                out_product(n_sup - 1, 1, j, groups=1)


def kernel(**inputs):
    import numpy as np
    import ml_dtypes
    import concourse.bacc as bacc
    from concourse.bass_utils import run_bass_kernel_spmd

    a = {k: np.asarray(v) for k, v in inputs.items()}
    w = {k[3:]: v for k, v in a.items() if k.startswith("L0_")}
    n = a["x"].shape[0]
    sups, grps, loads = n // SUP, n // (KG * P), n // (KL * P)

    def tiles(v):
        v = v.reshape(v.shape[0] // P, P, *v.shape[1:])
        return np.ascontiguousarray(np.moveaxis(v, 0, 1))

    def flat(v):
        return tiles(v).reshape(P, -1)

    xp = w["ffn_W_xproj"]
    xp4 = np.concatenate([xp[R:], xp[R:], xp[R:], xp[:R]], axis=0)
    arrays = {
        "adj_g": np.ascontiguousarray(
            a["adj"].reshape(sups, SUP, loads, KL, P).transpose(0, 2, 4, 3, 1)).reshape(sups, loads, P, KL * SUP),
        "x_tok": np.ascontiguousarray(a["x"].reshape(grps, KG, P, F).transpose(0, 2, 1, 3)).reshape(grps, P, KG * F),
        "x_fm": np.ascontiguousarray(a["x"].reshape(sups, SUP, FH, P).transpose(0, 3, 2, 1)),
        "gnn_w": tiles(w["gnn_weight"]),
        "w_fc1": tiles(w["ffn_W_fc1"]),
        "w_in_t": tiles(w["ffn_W_in"].T),
        "w_out": tiles(w["ffn_W_out"]),
        "w_fc2_t": tiles(w["ffn_W_fc2"].T),
        "w_xp_t": tiles(xp4.T),
        "w_dt_t": np.ascontiguousarray(w["ffn_W_dt"].T),
        "columns": np.concatenate([flat(w[k]) for k in (
            "ffn_conv_w", "ffn_conv_b", "ffn_D", "ffn_b_dt", "gnn_bias", "ffn_b_fc2", "ffn_b_fc1", "ffn_A_log")], axis=1),
        "ident_in": np.eye(P, dtype=np.float32),
        "behind_in": (np.arange(P)[:, None] >= np.array([[32, 64]])).astype(np.float32),
        "pick_in": np.tile(np.eye(R, dtype=np.float32), (3, 1)).astype(ml_dtypes.bfloat16),
    }
    nc = bacc.Bacc("TRN2", target_bir_lowering=False, num_devices=1, dynamic_dma_scratch_size=1024)
    aps = {k: nc.dram_tensor(k, v.shape, mybir.dt.from_np(v.dtype), kind="ExternalInput").ap() for k, v in arrays.items()}
    support = nc.dram_tensor("support", (grps, P, KG * F), F32, kind="Internal").ap()
    out = nc.dram_tensor("out", (2 * sups, P, FH, T), F32, kind="ExternalOutput").ap()
    graph_mamba_program(nc, **aps, support=support, out=out)
    got = run_bass_kernel_spmd(nc, [arrays], core_ids=[0]).results[0]["out"]
    return np.ascontiguousarray(got.transpose(0, 3, 2, 1)).reshape(n, F)
```

```python
from contextlib import ExitStack

import concourse.bass as bass
from concourse import mybir

P = 128
F32 = mybir.dt.float32
BF16 = mybir.dt.bfloat16
ALU = mybir.AluOpType
ACT = mybir.ActivationFunctionType
EPS = 1e-5

T = 256
SUP = 2 * T
KG = 4
KL = 2
RING = 4
F = 256
FH = F // P
DM = 512
DMT = DM // P
DI = 1024
E = DI // P
NS = 16
R = 32
TAPS = 4
HIST = TAPS - 1
PAIRS = NS // 2
SLOTS = E * PAIRS
PR_RING = 6

C_CONVW = 0
C_CONVB = C_CONVW + E * TAPS
C_D = C_CONVB + E
C_BDT = C_D + E
C_GB = C_BDT + E
C_B2 = C_GB + FH
C_B1 = C_B2 + FH
C_ALOG = C_B1 + DMT
C_ALL = C_ALOG + E * NS

G_MEAN, G_VAR, G_U, G_Z = 0, 1, 2, 2 + E // 2
G_XP = G_Z + E // 2
G_DT = G_XP + 1
G_BC = G_DT + E // 2
NP_ = G_BC + 2 * PAIRS

SUM_LAG = 3
HALVE_LAG = 3
AT_GATE = SUM_LAG
AT_OUT = 4
AT_STORE = 9
AT_GEND = 7
AT_GREAD = 10
AT_MEAN = 11
AT_G = 12
AT_VAR = 14
AT_RSTD = 15
AT_XN = 16
AT_U = 18
AT_Z = 26
AT_SILU = 34
AT_XP = 38
AT_XD = 43
AT_SPLIT = 44
AT_DT = 45
AT_BC = 57


def count(s, h, per, n):
    return s * (2 * per) + (h * per + n)


def is_halved(i):
    return i % 2 == 0 and i < SLOTS - HALVE_LAG - 1


def halved(i):
    return sum(map(is_halved, range(i)))


def back(i):
    if i >= PR_RING:
        return PR_RING
    return i + SLOTS - max(j for j in range(SLOTS) if j % PR_RING == i)


def tensor_work(i):
    w = 2 - is_halved((i - SUM_LAG) % SLOTS)
    w += 4 * (AT_OUT <= i < AT_OUT + 4)
    w += 2 * (i in (AT_MEAN, AT_VAR))
    w += 4 * (i in range(AT_U, AT_U + E, 2)) + 4 * (i in range(AT_Z, AT_Z + E, 2))
    w += 2 * (AT_XP <= i < AT_XP + 4) + 2 * (i in range(AT_DT, AT_DT + 3 * E // 2, 3))
    w += i >= AT_BC
    w -= SILU_SLACK * (AT_SILU < i <= AT_SILU + 2)
    return w


SILU_SLACK = 5


def gnn_schedule(n_mm):
    window = [*range(AT_G, SLOTS), *range(SLOTS), *range(AT_GEND)]
    level = (sum(map(tensor_work, window)) + 2 * n_mm) / len(window)
    done, total, ends = 0, 0.0, []
    for at, i in enumerate(window):
        total += tensor_work(i)
        while done < n_mm and total + 1 <= level * (at + 1):
            done, total = done + 1, total + 2
        ends.append(done)
    ends[-1] = n_mm
    return ends


def graph_mamba_program(nc, adj_g, x_tok, x_fm, gnn_w, w_fc1, w_in_t, w_out, w_fc2_t, w_xp_t, w_dt_t,
                        columns, ident_in, pick_in, behind_in, support, out):
    n_sup = adj_g.shape[0]
    n_ld = adj_g.shape[1]
    n_grp = x_tok.shape[0]
    n_mm = n_ld * KL * FH
    g_ends = gnn_schedule(n_mm)
    g_first = g_ends[SLOTS - AT_G - 1]
    ld_first = g_first // (KL * FH) + RING
    assert n_sup >= 4 and n_ld % RING == 0 and n_ld > 2 * RING and n_grp % 2 == 0 and n_ld * KL == n_grp * KG

    with ExitStack() as ctx:
        def sb(name, shape, dt=F32):
            return ctx.enter_context(nc.sbuf_tensor(name, shape, dt))

        def bank(name):
            return ctx.enter_context(nc.psum_tensor(name, [P, 512], F32))

        def sem(name):
            return ctx.enter_context(nc.semaphore(name))

        adj_sb = sb("adj_sb", [P, RING, KL * SUP])
        sup_sb = sb("sup_sb", [P, RING, KL * F])
        bc = sb("bc", [P, 2, PAIRS, 2 * T])
        x1n = sb("x1n", [P, FH, SUP])
        xin = sb("xin", [P, FH, SUP])
        hold = sb("hold", [P, 2, FH, T])
        xc = sb("xc", [P, FH, T])
        sq = sb("sq", [P, FH, T])
        rstd = sb("rstd", [P, T])
        u = sb("u", [P, 2, E, T])
        z = sb("z", [P, 2, E, T])
        delta = sb("delta", [P, 2, E, T])
        du = sb("du", [P, 2, E, T])
        uraw = sb("uraw", [P, E, HIST + T])
        y2 = sb("y2", [P, E, T])
        ytmp = sb("ytmp", [P, T])
        xd = sb("xd", [P, T])
        xr1 = sb("xr1", [P, T])
        xr2 = sb("xr2", [P, T])
        xs = sb("xs", [P, T], BF16)
        spa = sb("spa", [P, 2 * T])
        spw = sb("spw", [P, 2 * T])
        spl = sb("spl", [P, 2 * T])
        bx = sb("bx", [P, 4, 2 * T])
        pr = sb("pr", [P, PR_RING, 2 * T])
        state = sb("state", [P, E, NS])
        wc = sb("wc", [P, FH, 2 * DI])
        wo = sb("wo", [P, E, F])
        wxp = sb("wxp", [P, E, P])
        wdt = sb("wdt", [P, DI])
        cols = sb("cols", [P, C_ALL])
        a_neg = sb("a_neg", [P, E * NS])
        bcin = sb("bcin", [P, 2 * E])
        ident = sb("ident", [P, P])
        ones = sb("ones", [P, P])
        pick = sb("pick", [96, R], BF16)
        behind = sb("behind", [P, 2])
        eps = sb("eps", [P, 1])
        one = sb("one", [P, 1])
        ob = sb("ob", [P, FH, T])
        stats = sb("stats", [P, 2, KG, 6])
        mv = sb("mv", [P, 2, KG, 2])
        spare = sb("spare", [P, 1])
        rtok = sb("rtok", [P, 2, KG])
        win = bc[:, :, :, :].rearrange("p a b t -> p (a b t)").rearrange("p (k e) -> p k e", k=DMT)
        wout = du[:, :, :, :].rearrange("p a b t -> p (a b t)").rearrange("p (k e) -> p k e", k=DMT)
        wg = pr[:, 0, :].rearrange("p (f o) -> p f o", f=FH)
        wf1 = z[:, 0, 0:4, :]
        wf2 = z[:, 0, 4:8, :]
        xtok = [delta[:, t, 0:4, :] for t in range(2)]
        xnt = [u[:, t, :, :].rearrange("p e t -> p (e t)")[:, 0:FH * SUP].rearrange("p (f t) -> p f t", f=FH)
               for t in range(2)]
        sout = [y2[:, 4 * t:4 * t + 4, :] for t in range(2)]

        g_bank = [bank("g0"), bank("g1")]
        e_bank = [bank("e0"), bank("e1")]
        h_bank = [bank("h0"), bank("h1")]
        y_bank = bank("yb")
        m_bank = bank("mb")

        w_small = sem("w_small")
        w_big = sem("w_big")
        consts_set = sem("consts_set")
        a_set = sem("a_set")
        x_landed = [sem("x_landed0"), sem("x_landed1")]
        s_stats = sem("s_stats")
        s_var = sem("s_var")
        s_rstd = sem("s_rstd")
        s_xn = sem("s_xn")
        s_tr = sem("s_tr")
        s_trc = sem("s_trc")
        s_mm = sem("s_mm")
        s_out = sem("s_out")
        s_stored = [sem("s_stored0"), sem("s_stored1")]
        fold_mm = sem("fold_mm")
        fold_out = sem("fold_out")
        adj_landed = [sem(f"adj_landed{i}") for i in range(RING)]
        adj_used = sem("adj_used")
        xin_landed = sem("xin_landed")
        g_read = sem("g_read")
        p_mm = sem("p_mm")
        bc_done = sem("bc_done")
        ln_xc = sem("ln_xc")
        ln_sq = sem("ln_sq")
        ln_log = sem("ln_log")
        ln_rstd = sem("ln_rstd")
        ln_xn = sem("ln_xn")
        held = sem("held")
        u_raw = sem("u_raw")
        u_tap = sem("u_tap")
        u_conv = sem("u_conv")
        u_hist = sem("u_hist")
        z_raw = sem("z_raw")
        silu_done = sem("silu_done")
        xd_read = sem("xd_read")
        split = sem("split")
        sp_act = sem("sp_act")
        sp_dve = sem("sp_dve")
        sp_pool = sem("sp_pool")
        exp_done = sem("exp_done")
        bx_done = sem("bx_done")
        scan_done = sem("scan_done")
        pr_done = sem("pr_done")
        st_done = sem("st_done")
        st_zero = sem("st_zero")
        pr_halved = sem("pr_halved")
        sum_done = sem("sum_done")
        y_free = sem("y_free")
        y_done = sem("y_done")
        o_mm = sem("o_mm")
        o_free = sem("o_free")
        o_stored = sem("o_stored")

        SP_SMALL, SP_BIG = 9 * 16, 4 * 16
        SPLITS = 7
        FOLDS = FH * 4 + E // 2 + 1

        block = ctx.enter_context(nc.Block())

        @block.sync
        def _(sp):
            def load_x(q, t, wait):
                if wait is not None:
                    sp.wait_ge(s_tr, wait)
                sp.dma_start(xtok[t].rearrange("p a b -> p (a b)"), x_tok[q]).then_inc(x_landed[t], 16)

            def store_s(q, t):
                sp.wait_ge(s_out, q * 2 + 2)
                sp.dma_start(support[q], sout[t].rearrange("p a b -> p (a b)")).then_inc(s_stored[t], 16)

            load_x(0, 0, None)
            sp.dma_start(cols[:, :], columns).then_inc(w_small, 16)
            sp.dma_start(ident[:, :], ident_in).then_inc(w_small, 16)
            sp.dma_start(wg[:, :, :], gnn_w).then_inc(w_small, 16)
            load_x(1, 1, None)
            sp.dma_start(pick[:, :], pick_in).then_inc(w_small, 16)
            sp.dma_start(behind[:, :], behind_in).then_inc(w_small, 16)
            sp.dma_start(wxp[:, :, :], w_xp_t).then_inc(w_small, 16)
            sp.dma_start(wdt[P - R:P, :], w_dt_t).then_inc(w_small, 16)
            sp.dma_start(wf1, w_fc1).then_inc(w_small, 16)
            sp.dma_start(wf2, w_fc2_t).then_inc(w_small, 16)
            for k in range(DMT // 2):
                sp.dma_start(win[:, 2 * k:2 * k + 2, :], w_in_t[:, 2 * k:2 * k + 2, :]).then_inc(w_big, 16)
                sp.dma_start(wout[:, 2 * k:2 * k + 2, :], w_out[:, 2 * k:2 * k + 2, :]).then_inc(w_big, 16)
            with sp.Fori(0, n_grp // 2 - 1) as j:
                for t in range(2):
                    load_x(j * 2 + (2 + t), t, j * 2 + (1 + t))
                    store_s(j * 2 + t, t)
            for t in range(2):
                store_s(n_grp - 2 + t, t)

            def load_adj(s, r):
                if not (isinstance(s, int) and s * n_ld + r < RING):
                    sp.wait_ge(adj_used, s * n_ld + (r - RING + 1))
                sp.dma_start(adj_sb[:, r % RING, :], adj_g[s, r]).then_inc(adj_landed[r % RING], 16)
                if isinstance(s, int) and s == 0 and r < RING:
                    for t in range(2):
                        sp.wait_ge(s_stored[t], 8 * n_grp)
                sp.dma_start(sup_sb[:, r % RING, :], support[r * KL // KG][:, r * KL % KG * F:(r * KL % KG + KL) * F]).then_inc(adj_landed[r % RING], 16)

            def load_xin(s, wait):
                if wait:
                    sp.wait_ge(g_read, s * FH)
                sp.dma_start(xin[:, :, :], x_fm[s]).then_inc(xin_landed, 16)

            def store_out(s, h):
                sp.wait_ge(o_free, count(s, h, FH, FH))
                sp.dma_start(out[s * 2 + h], ob[:, :, :]).then_inc(o_stored, 16)

            def iteration(s, first=False, rest=True, begin=True):
                for r in range(ld_first, ld_first + 3):
                    if rest:
                        load_adj(s + 1, r)
                if not first:
                    store_out(s - 1, 1)
                for r in range(ld_first + 3, n_ld):
                    if rest:
                        load_adj(s + 1, r)
                for r in range(RING):
                    if begin:
                        load_adj(s + 2, r)
                store_out(s, 0)
                if begin:
                    load_xin(s + 2, True)
                for r in range(RING, ld_first):
                    if begin:
                        load_adj(s + 2, r)

            load_xin(0, False)
            for r in range(n_ld):
                load_adj(0, r)
            for r in range(ld_first):
                load_adj(1, r)
                if r == RING - 1:
                    load_xin(1, True)
            iteration(0, first=True)
            with sp.Fori(1, n_sup - 2) as s:
                iteration(s)
            iteration(n_sup - 2, begin=False)
            iteration(n_sup - 1, rest=False, begin=False)
            store_out(n_sup - 1, 1)
            sp.wait_ge(o_stored, 16 * 2 * n_sup)

        @block.gpsimd
        def _(pool):
            pool.memset(eps[:, :], EPS).then_inc(consts_set, 1)
            pool.memset(one[:, :], 1.0).then_inc(consts_set, 1)
            pool.memset(ones[:, :], 1.0 / F).then_inc(consts_set, 1)
            pool.memset(state[:, :, :], 0.0).then_inc(st_zero, 1)
            pool.memset(uraw[:, :, 0:HIST], 0.0).then_inc(st_zero, 1)

            pool.wait_ge(consts_set, 3)
            pool.wait_ge(w_small, SP_SMALL)

            def copy(dst, src):
                n, m = src.shape[0], src.shape[-1]
                lo = src.start_partition()
                by = one[lo:lo + n, :]
                by = by.to_broadcast([n, m]) if len(src.shape) == 2 else by.unsqueeze(1).to_broadcast(list(src.shape))
                return pool.tensor_tensor(dst, src, by, ALU.mult)

            def unit(s, h, i):
                d, np_ = divmod(i, PAIRS)
                if i == 0:
                    pool.wait_ge(sp_pool, count(s, h, E, E))
                if d == 0:
                    pool.wait_ge(bc_done, count(s, h, 2 * PAIRS, 2 * np_ + 1))
                if not (isinstance(s, int) and count(s, h, SLOTS, i) < 4):
                    pool.wait_ge(scan_done, count(s, h, 2 * SLOTS, 2 * (i - 3)))
                v = du[:, h, d, :].unsqueeze(1).to_broadcast([P, 2, T])
                pool.tensor_tensor(bx[:, i % 4, :].rearrange("p (a t) -> p a t", a=2), v,
                                   bc[:, 0, np_, :].rearrange("p (a t) -> p a t", a=2),
                                   ALU.mult).then_inc(bx_done, 1)

            def halve(s, h, i):
                pool.wait_ge(pr_done, count(s, h, SLOTS, i + 1))
                pr_i = pr[:, i % PR_RING, :]
                pool.tensor_tensor(pr_i[:, 0:T], pr_i[:, 0:T], pr_i[:, T:2 * T], ALU.add).then_inc(pr_halved, 1)

            def pieces(s, h, i):
                if i == AT_U + E + 1:
                    pool.wait_ge(u_conv, count(s, h, 3 * E, 3 * E))
                    tail, head = uraw[:, :, T:T + HIST], uraw[:, :, 0:HIST]
                    copy(head, tail).then_inc(u_hist, 1)
                if i == AT_SPLIT:
                    pool.wait_ge(xd_read, count(s, h, 1, 1))
                    copy(xs[:, :], xd[:, :]).then_inc(split, 1)
                    for n, (was, rest) in enumerate(((xd, xr1), (xr1, xr2))):
                        pool.wait_ge(split, count(s, h, SPLITS, 3 * n + 1))
                        by = behind[:, n:n + 1].to_broadcast([P, T])
                        pool.tensor_tensor(rest[:, :], xs[:, :], by, ALU.mult).then_inc(split, 1)
                        pool.wait_ge(split, count(s, h, SPLITS, 3 * n + 2))
                        pool.tensor_tensor(rest[:, :], was[:, :], rest[:, :], ALU.subtract).then_inc(split, 1)
                        pool.wait_ge(split, count(s, h, SPLITS, 3 * n + 3))
                        copy(xs[:, :], rest[:, :]).then_inc(split, 1)
                if i >= AT_DT + 3 and (i - AT_DT) % 3 == 0 and (i - AT_DT - 3) // 3 < E // 2:
                    b = (i - AT_DT - 3) // 3
                    pool.wait_ge(sp_dve, count(s, h, E, 2 * b + 2))
                    pool.wait_ge(sp_act, count(s, h, 3 * E, 6 * b + 6))
                    dl = delta[:, h, 2 * b:2 * b + 2, :].rearrange("p a t -> p (a t)")
                    pool.tensor_tensor(dl, dl, spl[:, :], ALU.add).then_inc(sp_pool, 1)
                    pool.wait_ge(sp_pool, count(s, h, E, 2 * b + 1))
                    pool.tensor_tensor(du[:, h, 2 * b:2 * b + 2, :].rearrange("p a t -> p (a t)"), dl,
                                       u[:, h, 2 * b:2 * b + 2, :].rearrange("p a t -> p (a t)"),
                                       ALU.mult).then_inc(sp_pool, 1)

            def chunk(s, h, following=True):
                for i in range(SLOTS):
                    unit(s, h, i)
                    if i >= HALVE_LAG and is_halved(i - HALVE_LAG):
                        halve(s, h, i - HALVE_LAG)
                    if following:
                        pieces(s + h, 1 - h, i)

            def iteration(s, following=True):
                chunk(s, 0)
                chunk(s, 1, following)

            for i in range(SLOTS):
                pieces(0, 0, i)
            iteration(0)
            with pool.Fori(1, n_sup - 2) as s:
                iteration(s)
            iteration(n_sup - 2)
            iteration(n_sup - 1, following=False)

        @block.scalar
        def _(act):
            act.preload_act_table_set("natural_log_exp_and_others")
            act.wait_ge(w_small, SP_SMALL)
            act.activation(a_neg[:, :], cols[:, C_ALOG:C_ALL], ACT.Exp).then_inc(a_set, 1)
            act.wait_ge(a_set, 1)
            act.activation(a_neg[:, :], a_neg[:, :], ACT.Identity, scale=-1.0).then_inc(a_set, 1)
            act.wait_ge(consts_set, 3)

            def rstd_tok(q, t):
                act.wait_ge(s_var, q + 1)
                act.activation(rtok[:, t, :], mv[:, t, :, 1], ACT.Ln, bias=eps[:, :]).then_inc(s_rstd, 1)
                act.wait_ge(s_rstd, q * 2 + 1)
                act.activation(rtok[:, t, :], rtok[:, t, :], ACT.Exp, scale=-0.5).then_inc(s_rstd, 1)

            def read_transposed(q, t, free):
                act.wait_ge(s_tr, q + 1)
                if free is not None:
                    act.wait_ge(s_mm, free)
                for f in range(FH):
                    act.activation(xnt[t][:, f, :], [e_bank, h_bank][t][f][:, :], ACT.Copy).then_inc(s_trc, 1)

            rstd_tok(0, 0)
            rstd_tok(1, 1)
            read_transposed(0, 0, None)
            rstd_tok(2, 0)
            read_transposed(1, 1, None)
            with act.Fori(1, n_grp // 2 - 1) as j:
                rstd_tok(j * 2 + 1, 1)
                read_transposed(j * 2, 0, j * 2 - 1)
                rstd_tok(j * 2 + 2, 0)
                read_transposed(j * 2 + 1, 1, j * 2)
            rstd_tok(n_grp - 1, 1)
            read_transposed(n_grp - 2, 0, n_grp - 3)
            read_transposed(n_grp - 1, 1, n_grp - 2)

            for n in range(FOLDS):
                src = [e_bank, h_bank][n // 2 % 2][n % 2]
                act.wait_ge(fold_mm, n + 1)
                if n < FH * 4:
                    act.activation(wc[:, n // 4, n % 4 * 512:n % 4 * 512 + 512], src[:, :], ACT.Copy).then_inc(fold_out, 1)
                elif n < FOLDS - 1:
                    d = 2 * (n - FH * 4)
                    act.activation(wo[:, d:d + 2, :].rearrange("p a t -> p (a t)"), src[:, :], ACT.Copy).then_inc(fold_out, 1)
                else:
                    act.activation(bcin[:, :], src[:, 0:2 * E], ACT.Copy).then_inc(fold_out, 1)

            def exps(s, h, i):
                d, np_ = divmod(i, PAIRS)
                if i == 0:
                    act.wait_ge(sp_pool, count(s, h, E, E))
                if not (isinstance(s, int) and count(s, h, SLOTS, i) < 2):
                    act.wait_ge(scan_done, count(s, h, 2 * SLOTS, 2 * (i - 1)))
                for a in range(2):
                    n = d * NS + 2 * np_ + a
                    ins = act.activation(e_bank[i % 2][:, a * T:(a + 1) * T], delta[:, h, d, :], ACT.Exp,
                                         scale=a_neg[:, n:n + 1])
                ins.then_inc(exp_done, 1)

            def pieces(s, h, i):
                half = slice(h * T, h * T + T)
                if i == AT_MEAN:
                    if not (isinstance(s, int) and s == 0):
                        act.wait_ge(o_free, count(s - 1, h, FH, FH))
                    act.wait_ge(g_read, s * FH + FH)
                    act.activation(hold[:, h, :, :], x1n[:, :, half], ACT.Copy).then_inc(held, 1)
                if i == AT_MEAN + 2:
                    act.wait_ge(ln_xc, count(s, h, 1, 1))
                    act.activation(sq[:, :, :], xc[:, :, :], ACT.Square).then_inc(ln_sq, 1)
                if i == AT_RSTD:
                    act.wait_ge(p_mm, count(s, h, NP_, G_VAR + 1))
                    act.activation(rstd[:, :], m_bank[:, 0:T], ACT.Ln, bias=eps[:, :]).then_inc(ln_log, 1)
                    act.wait_ge(ln_log, count(s, h, 1, 1))
                    act.activation(rstd[:, :], rstd[:, :], ACT.Exp, scale=-0.5).then_inc(ln_rstd, 1)
                for g in range(E // 2):
                    if i == AT_U + 2 * g + 1:
                        act.wait_ge(p_mm, count(s, h, NP_, G_U + g + 1))
                        if g == 0 and isinstance(s, int) and s == 0 and h == 0:
                            act.wait_ge(st_zero, 2)
                        elif g == 0:
                            act.wait_ge(u_hist, count(s, h, 1, 0))
                        for a in range(2):
                            e = 2 * g + a
                            act.activation(uraw[:, e, HIST:HIST + T], m_bank[:, a * T:(a + 1) * T], ACT.Identity,
                                           bias=bcin[:, e:e + 1]).then_inc(u_raw, 1)
                        act.wait_ge(u_raw, count(s, h, E, 2 * g + 2))
                        for a in range(2):
                            e = 2 * g + a
                            ins = act.activation(u[:, h, e, :], uraw[:, e, 0:T], ACT.Identity,
                                                 scale=cols[:, C_CONVW + e * TAPS:C_CONVW + e * TAPS + 1],
                                                 bias=cols[:, C_CONVB + e:C_CONVB + e + 1])
                            ins.then_inc(u_tap, 1)
                    if i == AT_Z + 2 * g + 1:
                        act.wait_ge(p_mm, count(s, h, NP_, G_Z + g + 1))
                        for a in range(2):
                            e = 2 * g + a
                            act.activation(z[:, h, e, :], m_bank[:, a * T:(a + 1) * T], ACT.Identity,
                                           bias=bcin[:, E + e:E + e + 1]).then_inc(z_raw, 1)
                    if i == AT_DT + 3 * g + 1:
                        c = count(s, h, 3 * E, 6 * g)
                        act.wait_ge(p_mm, count(s, h, NP_, G_DT + g + 1))
                        for a in range(2):
                            e = 2 * g + a
                            act.activation(delta[:, h, e, :], m_bank[:, a * T:(a + 1) * T], ACT.Identity,
                                           bias=cols[:, C_BDT + e:C_BDT + e + 1]).then_inc(sp_act, 1)
                        act.wait_ge(sp_act, c + 2)
                        again = not (isinstance(s, int) and s == 0 and h == 0 and g == 0)
                        if again:
                            act.wait_ge(sp_dve, count(s, h, E, 2 * g))
                        x2 = delta[:, h, 2 * g:2 * g + 2, :].rearrange("p a t -> p (a t)")
                        act.activation(spa[:, :], x2, ACT.Abs).then_inc(sp_act, 1)
                        act.wait_ge(sp_act, c + 3)
                        act.activation(spa[:, :], spa[:, :], ACT.Exp, scale=-1.0).then_inc(sp_act, 1)
                        act.wait_ge(sp_act, c + 4)
                        act.activation(spw[:, :], spa[:, :], ACT.Identity, bias=1.0).then_inc(sp_act, 1)
                        if again:
                            act.wait_ge(sp_pool, count(s, h, E, 2 * g - 1))
                        act.activation(spl[:, :], spa[:, :], ACT.Ln, bias=1.0).then_inc(sp_act, 1)
                if i == AT_SILU:
                    act.wait_ge(u_conv, count(s, h, 3 * E, 3 * E))
                    act.wait_ge(z_raw, count(s, h, E, E))
                    uu = u[:, h, :, :].rearrange("p a t -> p (a t)")
                    zz = z[:, h, :, :].rearrange("p a t -> p (a t)")
                    act.activation(uu, uu, ACT.Silu).then_inc(silu_done, 1)
                    act.activation(zz, zz, ACT.Silu).then_inc(silu_done, 1)
                    act.preload_act_table_set("natural_log_exp_and_others")
                if i >= AT_BC:
                    read_bc(s, h, i - AT_BC)

            def read_bc(s, h, np_):
                for w in range(2):
                    if not (isinstance(s, int) and s == 0 and h == 0):
                        act.wait_ge([bx_done, pr_done][w], count(s, h, SLOTS, np_ + 1 - PAIRS))
                    act.wait_ge(p_mm, count(s, h, NP_, G_BC + 2 * np_ + w + 1))
                    act.activation(bc[:, w, np_, :], m_bank[:, :], ACT.Copy).then_inc(bc_done, 1)

            def chunk(s, h, following=True):
                for i in range(SLOTS):
                    if i == 0:
                        read_bc(s, h, PAIRS - 1)
                    if i + 1 < SLOTS:
                        exps(s, h, i + 1)
                    elif following:
                        exps(s + h, 1 - h, 0)
                    if following:
                        pieces(s + h, 1 - h, i)

            def iteration(s, following=True):
                chunk(s, 0)
                chunk(s, 1, following)

            for i in range(SLOTS):
                pieces(0, 0, i)
            exps(0, 0, 0)
            iteration(0)
            with act.Fori(1, n_sup - 2) as s:
                iteration(s)
            iteration(n_sup - 2)
            iteration(n_sup - 1, following=False)

        @block.vector
        def _(dve):
            def stats_tok(q, t, landed):
                dve.wait_ge(x_landed[t], landed)
                for kt in range(KG):
                    dve.bn_stats(stats[:, t, kt, :], xtok[t][:, kt, :]).then_inc(s_stats, 1)
                dve.wait_ge(s_stats, q * KG + KG)
                dve.memset(spare[:, :], 0.0)
                for kt in range(KG):
                    ins = dve.bn_aggr(mv[:, t, kt, :], stats[:, t, kt, :])
                ins.then_inc(s_var, 1)

            def apply_tok(q, t):
                dve.wait_ge(s_rstd, q * 2 + 2)
                for kt in range(KG):
                    dve.tensor_scalar(xtok[t][:, kt, :], xtok[t][:, kt, :], mv[:, t, kt, 0:1], rtok[:, t, kt:kt + 1],
                                      ALU.subtract, ALU.mult).then_inc(s_xn, 1)

            def read_support(q, t, stored):
                dve.wait_ge(s_mm, q + 1)
                if stored is not None:
                    dve.wait_ge(s_stored[t], stored)
                for b in range(2):
                    src = [g_bank, [y_bank, m_bank]][t][b]
                    dve.tensor_copy(sout[t].rearrange("p a f -> p (a f)")[:, b * 512:b * 512 + 512],
                                    src[:, :]).then_inc(s_out, 1)

            stats_tok(0, 0, 16)
            apply_tok(0, 0)
            stats_tok(1, 1, 16)
            apply_tok(1, 1)
            read_support(0, 0, None)
            stats_tok(2, 0, 32)
            apply_tok(2, 0)
            read_support(1, 1, None)
            with dve.Fori(1, n_grp // 2 - 1) as j:
                stats_tok(j * 2 + 1, 1, j * 16 + 16)
                apply_tok(j * 2 + 1, 1)
                read_support(j * 2, 0, j * 16)
                stats_tok(j * 2 + 2, 0, j * 16 + 32)
                apply_tok(j * 2 + 2, 0)
                read_support(j * 2 + 1, 1, j * 16)
            stats_tok(n_grp - 1, 1, n_grp // 2 * 16)
            apply_tok(n_grp - 1, 1)
            read_support(n_grp - 2, 0, 8 * (n_grp - 2))
            read_support(n_grp - 1, 1, 8 * (n_grp - 2))

            dve.wait_ge(w_small, SP_SMALL)
            dve.wait_ge(st_zero, 2)

            def read_gnn(s):
                dve.wait_ge(adj_used, s * n_ld + n_ld)
                dve.wait_ge(xin_landed, s * 16 + 16)
                if not (isinstance(s, int) and s == 0):
                    dve.wait_ge(held, s * 2)
                    dve.wait_ge(ln_xc, s * 2)
                for f in range(FH):
                    dve.scalar_tensor_tensor(x1n[:, f, :], g_bank[f][:, :], cols[:, C_GB + f:C_GB + f + 1],
                                             xin[:, f, :], ALU.add, ALU.add).then_inc(g_read, 1)

            def unit_scan(s, h, i, a):
                d, np_ = divmod(i, PAIRS)
                if a == 0:
                    unit_ready(s, h, i)
                n = 2 * np_ + a
                dve.tensor_tensor_scan(h_bank[i % 2][:, a * T:(a + 1) * T], e_bank[i % 2][:, a * T:(a + 1) * T],
                                       bx[:, i % 4, a * T:(a + 1) * T], state[:, d, n:n + 1],
                                       ALU.mult, ALU.add).then_inc(scan_done, 1)

            def unit_ready(s, h, i):
                dve.wait_ge(exp_done, count(s, h, SLOTS, i + 1))
                dve.wait_ge(bx_done, count(s, h, SLOTS, i + 1))
                first = isinstance(s, int) and s == 0 and h == 0
                if not (first and i < 2):
                    dve.wait_ge(pr_done, count(s, h, SLOTS, i - 1))
                    dve.wait_ge(st_done, count(s, h, SLOTS, i - 1))

            def unit_mult(s, h, i):
                d, np_ = divmod(i, PAIRS)
                dve.wait_ge(scan_done, count(s, h, 2 * SLOTS, 2 * i + 2))
                if d == 0:
                    dve.wait_ge(bc_done, count(s, h, 2 * PAIRS, 2 * np_ + 2))
                if not (isinstance(s, int) and count(s, h, SLOTS, i) < back(i)):
                    dve.wait_ge(sum_done, count(s, h, SLOTS, i - back(i) + 1))
                dve.tensor_tensor(pr[:, i % PR_RING, :], h_bank[i % 2][:, :], bc[:, 1, np_, :], ALU.mult).then_inc(pr_done, 1)
                last = h_bank[i % 2][:, :].rearrange("p (a t) -> p a t", a=2)[:, :, T - 1]
                dve.tensor_copy(state[:, d, 2 * np_:2 * np_ + 2], last).then_inc(st_done, 1)

            def gate(s, h, d):
                dve.wait_ge(sum_done, count(s, h, SLOTS, (d + 1) * PAIRS))
                if d == 0 and not (isinstance(s, int) and s == 0 and h == 0):
                    dve.wait_ge(o_mm, count(s, h, 1, 0))
                if not (isinstance(s, int) and s == 0 and h == 0 and d == 0):
                    dve.wait_ge(y_done, count(s, h, E, d))
                dve.scalar_tensor_tensor(ytmp[:, :], u[:, h, d, :], cols[:, C_D + d:C_D + d + 1], y_bank[:, 0:T],
                                         ALU.mult, ALU.add).then_inc(y_free, 1)
                dve.wait_ge(y_free, count(s, h, E, d + 1))
                dve.tensor_tensor(y2[:, d, :], ytmp[:, :], z[:, h, d, :], ALU.mult).then_inc(y_done, 1)

            def finish(s, h):
                dve.wait_ge(o_mm, count(s, h, 1, 1))
                if not (isinstance(s, int) and s == 0 and h == 0):
                    dve.wait_ge(o_stored, count(s, h, 16, 0))
                for f in range(FH):
                    dve.scalar_tensor_tensor(ob[:, f, :], m_bank[:, f * T:(f + 1) * T], cols[:, C_B2 + f:C_B2 + f + 1],
                                             hold[:, h, f, :], ALU.add, ALU.add).then_inc(o_free, 1)

            def pieces(s, h, i):
                half = slice(h * T, h * T + T)
                if i == AT_MEAN + 1:
                    dve.wait_ge(p_mm, count(s, h, NP_, G_MEAN + 1))
                    m = m_bank[:, 0:T].unsqueeze(1).to_broadcast([P, FH, T])
                    dve.tensor_tensor(xc[:, :, :], x1n[:, :, half], m, ALU.subtract).then_inc(ln_xc, 1)
                if i == AT_XN:
                    dve.wait_ge(ln_rstd, count(s, h, 1, 1))
                    r = rstd[:, :].unsqueeze(1).to_broadcast([P, FH, T])
                    dve.tensor_tensor(xc[:, :, :], xc[:, :, :], r, ALU.mult).then_inc(ln_xn, 1)
                for g in range(E // 2):
                    if i == AT_U + 2 * g + 2:
                        dve.wait_ge(u_tap, count(s, h, E, 2 * g + 2))
                    if i in (AT_U + 2 * g + 2, AT_U + 2 * g + 3):
                        for n in range(3 * (i - AT_U - 2 * g - 2), 3 * (i - AT_U - 2 * g - 1)):
                            j, e = 1 + n // 2, 2 * g + n % 2
                            if n >= 2:
                                dve.wait_ge(u_conv, count(s, h, 3 * E, 6 * g + n - 1))
                            w = C_CONVW + e * TAPS + j
                            dve.scalar_tensor_tensor(u[:, h, e, :], uraw[:, e, j:j + T], cols[:, w:w + 1],
                                                     u[:, h, e, :], ALU.mult, ALU.add).then_inc(u_conv, 1)
                    if i == AT_DT + 3 * g + 2:
                        dve.wait_ge(sp_act, count(s, h, 3 * E, 6 * g + 5))
                        dve.scalar_tensor_tensor(spw[:, :], spw[:, :], -1.0, spa[:, :], ALU.add,
                                                 ALU.subtract).then_inc(sp_dve, 1)
                        dve.wait_ge(sp_dve, count(s, h, E, 2 * g + 1))
                        x2 = delta[:, h, 2 * g:2 * g + 2, :].rearrange("p a t -> p (a t)")
                        dve.scalar_tensor_tensor(x2, x2, 0.0, spw[:, :], ALU.max,
                                                 ALU.subtract).then_inc(sp_dve, 1)
                if i == AT_XD:
                    dve.wait_ge(p_mm, count(s, h, NP_, G_XP + 1))
                    dve.tensor_copy(xd[:, :], m_bank[:, 0:T]).then_inc(xd_read, 1)

            def chunk(s, h, before=True, following=True, gnn=True):
                for i in range(SLOTS):
                    unit_scan(s, h, i, 0)
                    if i > 0:
                        unit_mult(s, h, i - 1)
                    elif before:
                        unit_mult(s - 1 + h, 1 - h, SLOTS - 1)
                    unit_scan(s, h, i, 1)
                    if i % PAIRS == AT_GATE:
                        if i > PAIRS:
                            gate(s, h, i // PAIRS - 1)
                        elif before:
                            gate(s - 1 + h, 1 - h, E - 1)
                    if i == AT_STORE and before:
                        finish(s - 1 + h, 1 - h)
                    if i == AT_GREAD and h == 1 and gnn:
                        read_gnn(s + 1)
                    if following:
                        pieces(s + h, 1 - h, i)

            def iteration(s, before=True, following=True, gnn=True):
                chunk(s, 0, before=before)
                chunk(s, 1, following=following, gnn=gnn)

            read_gnn(0)
            for i in range(SLOTS):
                pieces(0, 0, i)
            iteration(0, before=False)
            with dve.Fori(1, n_sup - 2) as s:
                iteration(s)
            iteration(n_sup - 2)
            iteration(n_sup - 1, following=False, gnn=False)
            unit_mult(n_sup - 1, 1, SLOTS - 1)
            gate(n_sup - 1, 1, E - 1)
            finish(n_sup - 1, 1)

        @block.tensor
        def _(pe):
            pe.wait_ge(w_small, SP_SMALL)
            pe.wait_ge(consts_set, 3)

            def transposes(q, t, free):
                pe.wait_ge(s_xn, q * KG + KG)
                if free is not None:
                    pe.wait_ge(s_trc, free)
                for f in range(FH):
                    for kt in range(KG):
                        ins = pe.transpose([e_bank, h_bank][t][f][:, kt * P:(kt + 1) * P],
                                           xtok[t][:, kt, f * P:(f + 1) * P], ident[:, :])
                ins.then_inc(s_tr, 1)

            def products(q, t, free):
                pe.wait_ge(s_trc, q * 2 + 2)
                if free is not None:
                    pe.wait_ge(s_out, free)
                for kt in range(KG):
                    dst = [g_bank, [y_bank, m_bank]][t][kt // 2]
                    for f in range(FH):
                        ins = pe.matmul(dst[:, kt % 2 * F:kt % 2 * F + F], xnt[t][:, f, kt * P:(kt + 1) * P],
                                        wg[:, f, :], start=(f == 0), stop=(f == FH - 1))
                ins.then_inc(s_mm, 1)

            transposes(0, 0, None)
            transposes(1, 1, None)
            products(0, 0, None)
            transposes(2, 0, 2)
            products(1, 1, None)
            with pe.Fori(1, n_grp // 2 - 1) as j:
                transposes(j * 2 + 1, 1, j * 4)
                products(j * 2, 0, j * 4 - 2)
                transposes(j * 2 + 2, 0, j * 4 + 2)
                products(j * 2 + 1, 1, j * 4)
            transposes(n_grp - 1, 1, 2 * (n_grp - 2))
            products(n_grp - 2, 0, 2 * (n_grp - 3))
            products(n_grp - 1, 1, 2 * (n_grp - 2))

            pe.wait_ge(w_big, SP_BIG)
            for n in range(FOLDS):
                dst = [e_bank, h_bank][n // 2 % 2][n % 2]
                if n < 4:
                    pe.wait_ge(s_trc, 2 * n_grp)
                else:
                    pe.wait_ge(fold_out, n - 3)
                if n < FH * 4:
                    f, c = divmod(n, 4)
                    for k in range(DMT):
                        ins = pe.matmul(dst[:, :], wf1[:, k, f * P:(f + 1) * P], win[:, k, c * 512:(c + 1) * 512],
                                        start=(k == 0), stop=(k == DMT - 1))
                elif n < FOLDS - 1:
                    for a in range(2):
                        d = 2 * (n - FH * 4) + a
                        for k in range(DMT):
                            ins = pe.matmul(dst[:, a * F:(a + 1) * F], wout[:, k, d * P:(d + 1) * P], wf2[:, k, :],
                                            start=(k == 0), stop=(k == DMT - 1))
                else:
                    for e in range(2 * E):
                        for k in range(DMT):
                            ins = pe.matmul(dst[:, e:e + 1], win[:, k, e * P:(e + 1) * P],
                                            cols[:, C_B1 + k:C_B1 + k + 1], start=(k == 0), stop=(k == DMT - 1))
                ins.then_inc(fold_mm, 1)

            def gnn(s, lo, hi):
                for m in range(lo, hi):
                    kt, f = divmod(m, FH)
                    r = kt // KL
                    if m == 0:
                        if isinstance(s, int) and s == 0:
                            pe.wait_ge(s_out, 2 * n_grp)
                        else:
                            pe.wait_ge(g_read, s * FH)
                    if kt % KL == 0 and f == 0:
                        per = n_ld // RING * 32
                        pe.wait_ge(adj_landed[r % RING], s * per + 32 * (r // RING + 1))
                    ins = pe.matmul(g_bank[f][:, :],
                                    sup_sb[:, r % RING, kt % KL * F + f * P:kt % KL * F + (f + 1) * P],
                                    adj_sb[:, r % RING, kt % KL * SUP:(kt % KL + 1) * SUP],
                                    start=(kt == 0), stop=(kt == n_ld * KL - 1))
                    if kt % KL == KL - 1 and f == FH - 1:
                        ins.then_inc(adj_used, 1)

            def sums(s, h, i):
                d, np_ = divmod(i, PAIRS)
                first = isinstance(s, int) and s == 0 and h == 0
                if is_halved(i):
                    pe.wait_ge(pr_halved, count(s, h, halved(SLOTS), halved(i + 1)))
                else:
                    pe.wait_ge(pr_done, count(s, h, SLOTS, i + 1))
                if np_ == 0 and not (first and d == 0):
                    pe.wait_ge(y_free, count(s, h, E, d))
                parts = 1 if is_halved(i) else 2
                for a in range(parts):
                    ins = pe.matmul(y_bank[:, 0:T], ident[:, :], pr[:, i % PR_RING, a * T:(a + 1) * T],
                                    start=(np_ == 0 and a == 0), stop=(np_ == PAIRS - 1 and a == parts - 1))
                ins.then_inc(sum_done, 1)

            def out_product(s, h, j, groups=2):
                if j == 0:
                    pe.wait_ge(y_done, count(s, h, E, E))
                    pe.wait_ge(bc_done, count(s, h, 2 * PAIRS, 2 * PAIRS * groups))
                for n in range(4 * j, 4 * j + 4):
                    f, d = divmod(n, E)
                    ins = pe.matmul(m_bank[:, f * T:(f + 1) * T], wo[:, d, f * P:(f + 1) * P], y2[:, d, :],
                                    start=(d == 0), stop=(d == E - 1))
                if j == 3:
                    ins.then_inc(o_mm, 1)

            def pieces(s, h, i, before):
                half = slice(h * T, h * T + T)

                if i == AT_MEAN:
                    if before:
                        pe.wait_ge(o_free, count(s - 1, h, FH, FH))
                    elif not (isinstance(s, int) and s == 0 and h == 0):
                        pe.wait_ge(bc_done, count(s, h, 2 * PAIRS, 0))
                    pe.wait_ge(g_read, s * FH + FH)
                    for f in range(FH):
                        ins = pe.matmul(m_bank[:, 0:T], ones[:, :], x1n[:, f, half], start=(f == 0), stop=(f == FH - 1))
                    ins.then_inc(p_mm, 1)
                if i == AT_VAR:
                    pe.wait_ge(ln_sq, count(s, h, 1, 1))
                    for f in range(FH):
                        ins = pe.matmul(m_bank[:, 0:T], ones[:, :], sq[:, f, :], start=(f == 0), stop=(f == FH - 1))
                    ins.then_inc(p_mm, 1)
                for g in range(E // 2):
                    for at, base, off in ((AT_U, G_U, 0), (AT_Z, G_Z, E)):
                        if i == at + 2 * g:
                            if off == 0 and g == 0:
                                pe.wait_ge(ln_xn, count(s, h, 1, 1))
                            elif off == 0:
                                pe.wait_ge(u_raw, count(s, h, E, 2 * g))
                            elif g == 0:
                                pe.wait_ge(u_raw, count(s, h, E, E))
                            else:
                                pe.wait_ge(z_raw, count(s, h, E, 2 * g))
                            for a in range(2):
                                e = off + 2 * g + a
                                for f in range(FH):
                                    ins = pe.matmul(m_bank[:, a * T:(a + 1) * T], wc[:, f, e * P:(e + 1) * P], xc[:, f, :],
                                                    start=(f == 0), stop=(f == FH - 1))
                            ins.then_inc(p_mm, 1)
                    if i == AT_DT + 3 * g:
                        if g == 0:
                            pe.wait_ge(xd_read, count(s, h, 1, 1))
                        else:
                            pe.wait_ge(sp_act, count(s, h, 3 * E, 6 * g - 4))
                        for a in range(2):
                            e = 2 * g + a
                            ins = pe.matmul(m_bank[:, a * T:(a + 1) * T], wdt[P - R:P, e * P:(e + 1) * P], xd[P - R:P, :],
                                            start=True, stop=True)
                        ins.then_inc(p_mm, 1)
                if AT_XP <= i < AT_XP + 4:
                    if i == AT_XP:
                        pe.wait_ge(z_raw, count(s, h, E, E))
                        pe.wait_ge(silu_done, count(s, h, 2, 1))
                    for e in (2 * (i - AT_XP), 2 * (i - AT_XP) + 1):
                        ins = pe.matmul(m_bank[:, 0:T], wxp[:, e, :], u[:, h, e, :], start=(e == 0), stop=(e == E - 1))
                    if i == AT_XP + 3:
                        ins.then_inc(p_mm, 1)

            def spread(s, h, np_, w):
                if np_ == 0 and w == 0:
                    pe.wait_ge(split, count(s, h, SPLITS, SPLITS))
                    pe.wait_ge(sp_act, count(s, h, 3 * E, 3 * E - 4))
                else:
                    pe.wait_ge(bc_done, count(s, h, 2 * PAIRS, 2 * np_ + w))
                for a in range(2):
                    row = w * NS + 2 * np_ + a
                    ins = pe.matmul(m_bank[:, a * T:(a + 1) * T], pick[:, row:row + 1].to_broadcast([96, P]),
                                    xs[0:96, :], start=True, stop=True)
                ins.then_inc(p_mm, 1)

            def chunk(s, h, before=True, following=True, product=True, begin=True):
                for i in range(SLOTS):
                    if i == 0:
                        spread(s, h, PAIRS - 1, 0)
                    elif i >= AT_BC and following:
                        spread(s + h, 1 - h, i - AT_BC, 0)
                    if following:
                        pieces(s + h, 1 - h, i, before)
                    if before and AT_OUT <= i < AT_OUT + 4:
                        out_product(s - 1 + h, 1 - h, i - AT_OUT)
                    if i >= SUM_LAG:
                        sums(s, h, i - SUM_LAG)
                    elif before:
                        sums(s - 1 + h, 1 - h, SLOTS - SUM_LAG + i)

                    if i == 0:
                        spread(s, h, PAIRS - 1, 1)
                    elif i >= AT_BC and following:
                        spread(s + h, 1 - h, i - AT_BC, 1)
                    if product:
                        if h == 0:
                            at = SLOTS - AT_G + i
                            gnn(s + 1, g_ends[at - 1], g_ends[at])
                        elif i < AT_GEND:
                            at = 2 * SLOTS - AT_G + i
                            gnn(s + 1, g_ends[at - 1], g_ends[at])
                        elif i >= AT_G and begin:
                            at = i - AT_G
                            gnn(s + 2, g_ends[at - 1] if at else 0, g_ends[at])
            def iteration(s, before=True, following=True, product=True, begin=True):
                chunk(s, 0, before=before, product=product)
                chunk(s, 1, following=following, product=product, begin=begin)

            gnn(0, 0, n_mm)
            for i in range(SLOTS):
                pieces(0, 0, i, False)
                for w in range(2):
                    if i >= AT_BC:
                        spread(0, 0, i - AT_BC, w)
                gnn(1, i * g_first // SLOTS, (i + 1) * g_first // SLOTS)
            iteration(0, before=False)
            with pe.Fori(1, n_sup - 2) as s:
                iteration(s)
            iteration(n_sup - 2, begin=False)
            iteration(n_sup - 1, following=False, product=False)
            for i in range(SUM_LAG):
                sums(n_sup - 1, 1, SLOTS - SUM_LAG + i)
            for j in range(4):
                out_product(n_sup - 1, 1, j, groups=1)


def kernel(**inputs):
    import numpy as np
    import ml_dtypes
    import concourse.bacc as bacc
    from concourse.bass_utils import run_bass_kernel_spmd

    a = {k: np.asarray(v) for k, v in inputs.items()}
    w = {k[3:]: v for k, v in a.items() if k.startswith("L0_")}
    n = a["x"].shape[0]
    sups, grps, loads = n // SUP, n // (KG * P), n // (KL * P)

    def tiles(v):
        v = v.reshape(v.shape[0] // P, P, *v.shape[1:])
        return np.ascontiguousarray(np.moveaxis(v, 0, 1))

    def flat(v):
        return tiles(v).reshape(P, -1)

    xp = w["ffn_W_xproj"]
    xp4 = np.concatenate([xp[R:], xp[R:], xp[R:], xp[:R]], axis=0)
    arrays = {
        "adj_g": np.ascontiguousarray(
            a["adj"].reshape(sups, SUP, loads, KL, P).transpose(0, 2, 4, 3, 1)).reshape(sups, loads, P, KL * SUP),
        "x_tok": np.ascontiguousarray(a["x"].reshape(grps, KG, P, F).transpose(0, 2, 1, 3)).reshape(grps, P, KG * F),
        "x_fm": np.ascontiguousarray(a["x"].reshape(sups, SUP, FH, P).transpose(0, 3, 2, 1)),
        "gnn_w": tiles(w["gnn_weight"]),
        "w_fc1": tiles(w["ffn_W_fc1"]),
        "w_in_t": tiles(w["ffn_W_in"].T),
        "w_out": tiles(w["ffn_W_out"]),
        "w_fc2_t": tiles(w["ffn_W_fc2"].T),
        "w_xp_t": tiles(xp4.T),
        "w_dt_t": np.ascontiguousarray(w["ffn_W_dt"].T),
        "columns": np.concatenate([flat(w[k]) for k in (
            "ffn_conv_w", "ffn_conv_b", "ffn_D", "ffn_b_dt", "gnn_bias", "ffn_b_fc2", "ffn_b_fc1", "ffn_A_log")], axis=1),
        "ident_in": np.eye(P, dtype=np.float32),
        "behind_in": (np.arange(P)[:, None] >= np.array([[32, 64]])).astype(np.float32),
        "pick_in": np.tile(np.eye(R, dtype=np.float32), (3, 1)).astype(ml_dtypes.bfloat16),
    }
    nc = bacc.Bacc("TRN2", target_bir_lowering=False, num_devices=1, dynamic_dma_scratch_size=1024)
    aps = {k: nc.dram_tensor(k, v.shape, mybir.dt.from_np(v.dtype), kind="ExternalInput").ap() for k, v in arrays.items()}
    support = nc.dram_tensor("support", (grps, P, KG * F), F32, kind="Internal").ap()
    out = nc.dram_tensor("out", (2 * sups, P, FH, T), F32, kind="ExternalOutput").ap()
    graph_mamba_program(nc, **aps, support=support, out=out)
    got = run_bass_kernel_spmd(nc, [arrays], core_ids=[0]).results[0]["out"]
    return np.ascontiguousarray(got.transpose(0, 3, 2, 1)).reshape(n, F)
```

```python
from contextlib import ExitStack

import concourse.bass as bass
from concourse import mybir

P = 128
F32 = mybir.dt.float32
BF16 = mybir.dt.bfloat16
ALU = mybir.AluOpType
ACT = mybir.ActivationFunctionType
EPS = 1e-5

T = 256
SUP = 2 * T
KG = 4
KL = 2
RING = 4
F = 256
FH = F // P
DM = 512
DMT = DM // P
DI = 1024
E = DI // P
NS = 16
R = 32
TAPS = 4
HIST = TAPS - 1
PAIRS = NS // 2
SLOTS = E * PAIRS
PR_RING = 8
EX_RING = 4
BX_RING = 8
EX_AHEAD = 3
BX_AHEAD = 4

C_CONVW = 0
C_CONVB = C_CONVW + E * TAPS
C_D = C_CONVB + E
C_BDT = C_D + E
C_GB = C_BDT + E
C_B2 = C_GB + FH
C_B1 = C_B2 + FH
C_ALOG = C_B1 + DMT
C_ALL = C_ALOG + E * NS

G_MEAN, G_VAR, G_U, G_Z = 0, 1, 2, 2 + E // 2
G_XP = G_Z + E // 2
G_DT = G_XP + 1
G_BC = G_DT + E // 2 - 1
G_DT_LAST = G_BC + 2 * PAIRS
GROUPS = G_DT_LAST + 1
G_O = GROUPS
assert (G_O + 1) % 2 == 0

SUM_LAG = 4
HALVE_LAG = 3
AT_GATE = SUM_LAG + 1
AT_OUT = AT_GATE + 1
AT_STORE = AT_OUT + 5
AT_GEND = 7
AT_GREAD = 10
AT_G = 12
AT_MEAN = 11
AT_VAR = 14
AT_RSTD = 15
AT_XN = 16
AT_U = 18
AT_TAPS = AT_U + 3
AT_Z = 26
AT_SILU = 34
AT_XP = 39
AT_XD = 44
AT_SPLIT = 45
AT_DT = 46
AT_BC = 57
BC_OVER = AT_BC + PAIRS - SLOTS
AT_DT_LAST = BC_OVER
LAST_SLACK = 3


def count(s, h, per, n):
    return s * (2 * per) + (h * per + n)


def is_halved(i):
    if i >= SLOTS - HALVE_LAG - 1:
        return False
    if i < AT_SPLIT + 3:
        return i % 16 != 3
    return i % 2 == 0 and i >= AT_BC - 2


def halved(i):
    return sum(map(is_halved, range(i)))


def dt_group(g):
    return G_DT + g if g < E // 2 - 1 else G_DT_LAST


def tensor_work(i):
    w = 2 - is_halved((i - SUM_LAG) % SLOTS)
    w += 4 * (AT_OUT <= i < AT_OUT + 4)
    w += 2 * (i in (AT_MEAN, AT_VAR))
    w += 4 * (i in range(AT_U, AT_U + E, 2)) + 4 * (i in range(AT_Z, AT_Z + E, 2))
    w += 2 * (AT_XP <= i < AT_XP + 4) + 2 * (i in range(AT_DT, AT_DT + 3 * (E // 2 - 1), 3) or i == AT_DT_LAST)
    w += i >= AT_BC or i < BC_OVER
    return w


def vector_work(i):
    w = 6
    w += 1.7 * (i % PAIRS == AT_GATE) + 1.4 * (i == AT_STORE) + 1.6 * (i == AT_GREAD)
    w += 1.4 * (i in (AT_MEAN + 1, AT_XN))
    w += 2.8 * (AT_TAPS <= i < AT_TAPS + E - 2 or AT_SILU <= i < AT_SILU + 2)
    w += 2.8 * (i - 3 in range(AT_DT, AT_DT + 3 * (E // 2 - 1), 3) or i - 3 - LAST_SLACK == AT_DT_LAST)
    return w


def gnn_schedule(n_mm):
    window = [*range(AT_G, SLOTS), *range(SLOTS), *range(AT_GEND)]
    level = (sum(map(tensor_work, window)) + 2 * n_mm) / sum(map(vector_work, window))
    done, total, target, ends = 0, 0.0, 0.0, []
    for i in window:
        total += tensor_work(i)
        target += level * vector_work(i)
        while done < n_mm and total + 1 <= target:
            done, total = done + 1, total + 2
        ends.append(done)
    ends[-1] = n_mm
    return ends


def graph_mamba_program(nc, adj_g, x_tok, x_fm, gnn_w, w_fc1, w_in_t, w_out, w_fc2_t, w_xp_t, w_dt_t,
                        columns, ident_in, pick_in, behind_in, support, out):
    n_sup = adj_g.shape[0]
    n_ld = adj_g.shape[1]
    n_grp = x_tok.shape[0]
    n_mm = n_ld * KL * FH
    g_ends = gnn_schedule(n_mm)
    g_first = g_ends[SLOTS - AT_G - 1]
    ld_first = g_first // (KL * FH) + RING
    assert n_sup >= 4 and n_grp > 10 and n_ld % RING == 0 and n_ld > 2 * RING
    assert n_grp % 2 == 0 and n_ld * KL == n_grp * KG

    with ExitStack() as ctx:
        def sb(name, shape, dt=F32):
            return ctx.enter_context(nc.sbuf_tensor(name, shape, dt))

        def bank(name):
            return ctx.enter_context(nc.psum_tensor(name, [P, 512], F32))

        def sem(name):
            return ctx.enter_context(nc.semaphore(name))

        adj_sb = sb("adj_sb", [P, RING, KL * SUP])
        sup_sb = sb("sup_sb", [P, RING, KL * F])
        bc = sb("bc", [P, 2, PAIRS, 2 * T])
        x1n = sb("x1n", [P, FH, SUP])
        xin = sb("xin", [P, FH, SUP])
        hold = sb("hold", [P, 2, FH, T])
        xc = sb("xc", [P, FH, T])
        rstd = sb("rstd", [P, T])
        u = sb("u", [P, 2, E, T])
        z = sb("z", [P, 2, E, T])
        delta = sb("delta", [P, E, T])
        du = sb("du", [P, E, T])
        uraw = sb("uraw", [P, E, HIST + T])
        y2 = sb("y2", [P, E, T])
        ytmp = sb("ytmp", [P, T])
        xd = sb("xd", [P, T])
        xr1, xr2 = xc[:, 0, :], xc[:, 1, :]
        xs = sb("xs", [P, T], BF16)
        spa = sb("spa", [P, 2 * T])
        sq = spa[:, :].rearrange("p (f t) -> p f t", f=FH)
        spw = sb("spw", [P, 2 * T])
        spl = sb("spl", [P, 2 * T])
        ex = sb("ex", [P, EX_RING, 2 * T])
        bx = sb("bx", [P, BX_RING, 2 * T])
        pr = sb("pr", [P, PR_RING, 2 * T])
        state = sb("state", [P, E, NS])
        wc = sb("wc", [P, FH, 2 * DI])
        wo = sb("wo", [P, E, F])
        wxp = sb("wxp", [P, E, P])
        wdt = sb("wdt", [P, DI])
        cols = sb("cols", [P, C_ALL])
        a_neg = sb("a_neg", [P, E * NS])
        bcin = sb("bcin", [P, 2 * E])
        ident = sb("ident", [P, P])
        ones = sb("ones", [P, P])
        pick = sb("pick", [96, R], BF16)
        behind = sb("behind", [P, 2])
        eps = sb("eps", [P, 1])
        one = sb("one", [P, 1])
        ob = sb("ob", [P, FH, T])
        stats = sb("stats", [P, 2, KG, 6])
        mv = sb("mv", [P, 2, KG, 2])
        spare = sb("spare", [P, 1])
        rtok = sb("rtok", [P, 2, KG])
        win = bc[:, :, :, :].rearrange("p a b t -> p (a b t)").rearrange("p (k e) -> p k e", k=DMT)
        wout = bx[:, :, :].rearrange("p a t -> p (a t)").rearrange("p (k e) -> p k e", k=DMT)
        wg = pr[:, 0, :].rearrange("p (f o) -> p f o", f=FH)
        wf1 = z[:, 0, 0:4, :]
        wf2 = z[:, 0, 4:8, :]
        xtok = [delta[:, 4 * t:4 * t + 4, :] for t in range(2)]
        xnt = [u[:, t, :, :].rearrange("p e t -> p (e t)")[:, 0:FH * SUP].rearrange("p (f t) -> p f t", f=FH)
               for t in range(2)]
        sout = [y2[:, 4 * t:4 * t + 4, :] for t in range(2)]

        g_bank = [bank("g0"), bank("g1")]
        h_bank = [bank("h0"), bank("h1")]
        y_bank = [bank("y0"), bank("y1")]
        m_bank = [bank("m0"), bank("m1")]

        w_small = sem("w_small")
        w_big = sem("w_big")
        consts_set = sem("consts_set")
        a_set = sem("a_set")
        x_landed = [sem("x_landed0"), sem("x_landed1")]
        s_stats = sem("s_stats")
        s_var = sem("s_var")
        s_rstd = sem("s_rstd")
        s_xn = sem("s_xn")
        s_tr = sem("s_tr")
        s_trc = sem("s_trc")
        s_mm = sem("s_mm")
        s_out = sem("s_out")
        s_stored = [sem("s_stored0"), sem("s_stored1")]
        fold_mm = sem("fold_mm")
        fold_out = sem("fold_out")
        adj_landed = [sem(f"adj_landed{i}") for i in range(RING)]
        adj_used = sem("adj_used")
        xin_landed = sem("xin_landed")
        g_read = sem("g_read")
        p_mm = sem("p_mm")
        bc_done = sem("bc_done")
        ln_xc = sem("ln_xc")
        ln_sq = sem("ln_sq")
        ln_log = sem("ln_log")
        ln_rstd = sem("ln_rstd")
        ln_xn = sem("ln_xn")
        held = sem("held")
        u_raw = sem("u_raw")
        u_tap = sem("u_tap")
        u_conv = sem("u_conv")
        u_hist = sem("u_hist")
        z_raw = sem("z_raw")
        silu_done = sem("silu_done")
        xd_read = sem("xd_read")
        split = sem("split")
        sp_act = sem("sp_act")
        sp_dve = sem("sp_dve")
        sp_pool = sem("sp_pool")
        exp_done = sem("exp_done")
        bx_done = sem("bx_done")
        scan_done = sem("scan_done")
        pr_done = sem("pr_done")
        st_done = sem("st_done")
        st_zero = sem("st_zero")
        pr_halved = sem("pr_halved")
        sum_done = sem("sum_done")
        y_free = sem("y_free")
        y_done = sem("y_done")
        o_mm = sem("o_mm")
        o_free = sem("o_free")
        o_stored = sem("o_stored")

        SP_SMALL, SP_BIG = 7 * 16, 6 * 16
        SPLITS = 7
        FOLDS = FH * 4 + E // 2 + 1

        block = ctx.enter_context(nc.Block())

        @block.sync
        def _(sp):
            def load_x(q, t, wait):
                if wait is not None:
                    sp.wait_ge(s_tr, wait)
                sp.dma_start(xtok[t].rearrange("p a b -> p (a b)"), x_tok[q]).then_inc(x_landed[t], 16)

            def store_s(q, t):
                sp.wait_ge(s_out, q * 2 + 2)
                sp.dma_start(support[q], sout[t].rearrange("p a b -> p (a b)")).then_inc(s_stored[t], 16)

            load_x(0, 0, None)
            sp.dma_start(cols[:, :], columns).then_inc(w_small, 16)
            sp.dma_start(ident[:, :], ident_in).then_inc(w_small, 16)
            sp.dma_start(wg[:, :, :], gnn_w).then_inc(w_small, 16)
            load_x(1, 1, None)
            sp.dma_start(pick[:, :], pick_in).then_inc(w_small, 16)
            sp.dma_start(behind[:, :], behind_in).then_inc(w_small, 16)
            sp.dma_start(wxp[:, :, :], w_xp_t).then_inc(w_small, 16)
            sp.dma_start(wdt[P - R:P, :], w_dt_t).then_inc(w_small, 16)
            load_x(2, 0, 1)
            fold_loads = [(wf1, w_fc1), (wf2, w_fc2_t)]
            for k in (slice(0, DMT // 2), slice(DMT // 2, DMT)):
                fold_loads += [(win[:, k, :], w_in_t[:, k, :]), (wout[:, k, :], w_out[:, k, :])]
            peeled = len(fold_loads) // 2
            for j in range(peeled):
                for t in range(2):
                    load_x(j * 2 + (3 + t), 1 - t, j * 2 + (2 + t))
                    sp.dma_start(*fold_loads[j * 2 + t]).then_inc(w_big, 16)
                    store_s(j * 2 + t, t)
            with sp.Fori(peeled, n_grp // 2 - 2) as j:
                for t in range(2):
                    load_x(j * 2 + (3 + t), 1 - t, j * 2 + (2 + t))
                    store_s(j * 2 + t, t)
            load_x(n_grp - 1, 1, n_grp - 2)
            for q in range(n_grp - 4, n_grp):
                store_s(q, q % 2)

            def load_adj(s, r):
                if not (isinstance(s, int) and s * n_ld + r < RING):
                    sp.wait_ge(adj_used, s * n_ld + (r - RING + 1))
                sp.dma_start(adj_sb[:, r % RING, :], adj_g[s, r]).then_inc(adj_landed[r % RING], 16)
                if isinstance(s, int) and s == 0 and r < RING:
                    for t in range(2):
                        sp.wait_ge(s_stored[t], 8 * n_grp)
                sp.dma_start(sup_sb[:, r % RING, :],
                             support[r * KL // KG][:, r * KL % KG * F:(r * KL % KG + KL) * F]).then_inc(adj_landed[r % RING], 16)

            def load_xin(s, wait):
                if wait:
                    sp.wait_ge(g_read, s * FH)
                sp.dma_start(xin[:, :, :], x_fm[s]).then_inc(xin_landed, 16)

            def store_out(s, h):
                sp.wait_ge(o_free, count(s, h, 1, 1))
                sp.dma_start(out[s * 2 + h], ob[:, :, :]).then_inc(o_stored, 16)

            def iteration(s, first=False, rest=True, begin=True):
                for r in range(ld_first, ld_first + 3):
                    if rest:
                        load_adj(s + 1, r)
                if not first:
                    store_out(s - 1, 1)
                for r in range(ld_first + 3, n_ld):
                    if rest:
                        load_adj(s + 1, r)
                for r in range(RING):
                    if begin:
                        load_adj(s + 2, r)
                store_out(s, 0)
                if begin:
                    load_xin(s + 2, True)
                for r in range(RING, ld_first):
                    if begin:
                        load_adj(s + 2, r)

            load_xin(0, False)
            for r in range(n_ld):
                load_adj(0, r)
            for r in range(ld_first):
                load_adj(1, r)
                if r == RING - 1:
                    load_xin(1, True)
            iteration(0, first=True)
            with sp.Fori(1, n_sup - 2) as s:
                iteration(s)
            iteration(n_sup - 2, begin=False)
            iteration(n_sup - 1, rest=False, begin=False)
            store_out(n_sup - 1, 1)
            sp.wait_ge(o_stored, 16 * 2 * n_sup)

        @block.gpsimd
        def _(pool):
            pool.memset(eps[:, :], EPS).then_inc(consts_set, 1)
            pool.memset(one[:, :], 1.0).then_inc(consts_set, 1)
            pool.memset(ones[:, :], 1.0 / F).then_inc(consts_set, 1)
            pool.memset(state[:, :, :], 0.0).then_inc(st_zero, 1)
            pool.memset(uraw[:, :, 0:HIST], 0.0).then_inc(st_zero, 1)

            pool.wait_ge(consts_set, 3)
            pool.wait_ge(w_small, SP_SMALL)

            def copy(dst, src):
                n, m = src.shape[0], src.shape[-1]
                lo = src.start_partition()
                by = one[lo:lo + n, :]
                by = by.to_broadcast([n, m]) if len(src.shape) == 2 else by.unsqueeze(1).to_broadcast(list(src.shape))
                return pool.tensor_tensor(dst, src, by, ALU.mult)

            def unit(s, h, i):
                d, np_ = divmod(i, PAIRS)
                if i % (2 * PAIRS) == 0:
                    pool.wait_ge(sp_pool, count(s, h, E, 2 * (d // 2) + 2))
                if d == 0:
                    pool.wait_ge(bc_done, count(s, h, 2 * PAIRS, 2 * np_ + 1))
                if not (isinstance(s, int) and count(s, h, SLOTS, i) < BX_RING):
                    pool.wait_ge(scan_done, count(s, h, 2 * SLOTS, 2 * (i - BX_RING + 1)))
                v = du[:, d, :].unsqueeze(1).to_broadcast([P, 2, T])
                pool.tensor_tensor(bx[:, i % BX_RING, :].rearrange("p (a t) -> p a t", a=2), v,
                                   bc[:, 0, np_, :].rearrange("p (a t) -> p a t", a=2),
                                   ALU.mult).then_inc(bx_done, 1)

            def halve(s, h, i):
                pool.wait_ge(pr_done, count(s, h, SLOTS, i + 1))
                pr_i = pr[:, i % PR_RING, :]
                pool.tensor_tensor(pr_i[:, 0:T], pr_i[:, 0:T], pr_i[:, T:2 * T], ALU.add).then_inc(pr_halved, 1)

            def pieces(s, h, i):
                if i == AT_SILU + 3:
                    pool.wait_ge(u_conv, count(s, h, 3 * E, 3 * E))
                    tail, head = uraw[:, :, T:T + HIST], uraw[:, :, 0:HIST]
                    copy(head, tail).then_inc(u_hist, 1)
                if i in (AT_SPLIT + 2, AT_SPLIT + 5):
                    was, rest = (xd[:, :], xr1) if i == AT_SPLIT + 2 else (xr1, xr2)
                    pool.wait_ge(split, count(s, h, SPLITS, i - AT_SPLIT))
                    pool.tensor_tensor(rest, was, rest, ALU.subtract).then_inc(split, 1)
                for g in range(E // 2 - 1):
                    softplus(s, h, g, i - AT_DT - 3 * g)

            def softplus(s, h, g, step):
                dl = delta[:, 2 * g:2 * g + 2, :].rearrange("p a t -> p (a t)")
                if step == 4:
                    pool.wait_ge(sp_dve, count(s, h, E, 2 * g + 2))
                    pool.wait_ge(sp_act, count(s, h, 3 * E, 6 * g + 6))
                    pool.tensor_tensor(dl, dl, spl[:, :], ALU.add).then_inc(sp_pool, 1)
                if step == 5:
                    pool.wait_ge(sp_pool, count(s, h, E, 2 * g + 1))
                    pool.tensor_tensor(du[:, 2 * g:2 * g + 2, :].rearrange("p a t -> p (a t)"), dl,
                                       u[:, h, 2 * g:2 * g + 2, :].rearrange("p a t -> p (a t)"),
                                       ALU.mult).then_inc(sp_pool, 1)

            def chunk(s, h, following=True):
                for i in range(SLOTS):
                    if i + BX_AHEAD < SLOTS:
                        unit(s, h, i + BX_AHEAD)
                    elif following:
                        unit(s + h, 1 - h, i + BX_AHEAD - SLOTS)
                    softplus(s, h, E // 2 - 1, i - LAST_SLACK - AT_DT_LAST)
                    if i >= HALVE_LAG and is_halved(i - HALVE_LAG):
                        halve(s, h, i - HALVE_LAG)
                    if following:
                        pieces(s + h, 1 - h, i)

            def iteration(s, following=True):
                chunk(s, 0)
                chunk(s, 1, following)

            for i in range(SLOTS):
                pieces(0, 0, i)
            for i in range(BX_AHEAD):
                unit(0, 0, i)
            iteration(0)
            with pool.Fori(1, n_sup - 2) as s:
                iteration(s)
            iteration(n_sup - 2)
            iteration(n_sup - 1, following=False)

        @block.scalar
        def _(act):
            act.preload_act_table_set("natural_log_exp_and_others")
            act.wait_ge(w_small, SP_SMALL)
            act.activation(a_neg[:, :], cols[:, C_ALOG:C_ALL], ACT.Exp).then_inc(a_set, 1)
            act.wait_ge(a_set, 1)
            act.activation(a_neg[:, :], a_neg[:, :], ACT.Identity, scale=-1.0).then_inc(a_set, 1)
            act.wait_ge(consts_set, 3)

            def rstd_tok(q, t):
                act.wait_ge(s_var, q + 1)
                act.activation(rtok[:, t, :], mv[:, t, :, 1], ACT.Ln, bias=eps[:, :]).then_inc(s_rstd, 1)
                act.wait_ge(s_rstd, q * 2 + 1)
                act.activation(rtok[:, t, :], rtok[:, t, :], ACT.Exp, scale=-0.5).then_inc(s_rstd, 1)

            def read_transposed(q, t, free):
                act.wait_ge(s_tr, q + 1)
                if free is not None:
                    act.wait_ge(s_mm, free)
                for f in range(FH):
                    act.activation(xnt[t][:, f, :], [m_bank, h_bank][t][f][:, :], ACT.Copy).then_inc(s_trc, 1)

            rstd_tok(0, 0)
            rstd_tok(1, 1)
            read_transposed(0, 0, None)
            rstd_tok(2, 0)
            read_transposed(1, 1, None)
            with act.Fori(1, n_grp // 2 - 1) as j:
                rstd_tok(j * 2 + 1, 1)
                read_transposed(j * 2, 0, j * 2 - 1)
                rstd_tok(j * 2 + 2, 0)
                read_transposed(j * 2 + 1, 1, j * 2)
            rstd_tok(n_grp - 1, 1)
            read_transposed(n_grp - 2, 0, n_grp - 3)
            read_transposed(n_grp - 1, 1, n_grp - 2)

            for n in range(FOLDS):
                src = [m_bank, h_bank][n // 2 % 2][n % 2]
                act.wait_ge(fold_mm, n + 1)
                if n < FH * 4:
                    act.activation(wc[:, n // 4, n % 4 * 512:n % 4 * 512 + 512], src[:, :], ACT.Copy).then_inc(fold_out, 1)
                elif n < FOLDS - 1:
                    d = 2 * (n - FH * 4)
                    act.activation(wo[:, d:d + 2, :].rearrange("p a t -> p (a t)"), src[:, :], ACT.Copy).then_inc(fold_out, 1)
                else:
                    act.activation(bcin[:, :], src[:, 0:2 * E], ACT.Copy).then_inc(fold_out, 1)

            def exps(s, h, i):
                d, np_ = divmod(i, PAIRS)
                if i % (2 * PAIRS) == 0:
                    act.wait_ge(sp_pool, count(s, h, E, 2 * (d // 2) + 1))
                if not (isinstance(s, int) and count(s, h, SLOTS, i) < EX_RING):
                    act.wait_ge(scan_done, count(s, h, 2 * SLOTS, 2 * (i - EX_RING + 1)))
                for a in range(2):
                    n = d * NS + 2 * np_ + a
                    ins = act.activation(ex[:, i % EX_RING, a * T:(a + 1) * T], delta[:, d, :], ACT.Exp,
                                         scale=a_neg[:, n:n + 1])
                ins.then_inc(exp_done, 1)

            def pieces(s, h, i):
                half = slice(h * T, h * T + T)
                if i == AT_MEAN:
                    if not (isinstance(s, int) and s == 0):
                        act.wait_ge(o_free, count(s - 1, h, 1, 1))
                    act.wait_ge(g_read, s * FH + FH)
                    for f in range(FH):
                        ins = act.activation(hold[:, h, f, :], x1n[:, f, half], ACT.Identity,
                                             bias=cols[:, C_B2 + f:C_B2 + f + 1])
                    ins.then_inc(held, 1)
                if i == AT_MEAN + 2:
                    act.wait_ge(ln_xc, count(s, h, 1, 1))
                    if not (isinstance(s, int) and s == 0 and h == 0):
                        act.wait_ge(sp_dve, count(s, h, E, -1))
                    act.activation(sq[:, :, :], xc[:, :, :], ACT.Square).then_inc(ln_sq, 1)
                if i == AT_RSTD:
                    act.wait_ge(p_mm, count(s, h, GROUPS, G_VAR + 1))
                    act.activation(rstd[:, :], m_bank[G_VAR % 2][:, 0:T], ACT.Ln, bias=eps[:, :]).then_inc(ln_log, 1)
                    act.wait_ge(ln_log, count(s, h, 1, 1))
                    act.activation(rstd[:, :], rstd[:, :], ACT.Exp, scale=-0.5).then_inc(ln_rstd, 1)
                for g in range(E // 2):
                    if i == AT_U + 2 * g + 1:
                        act.wait_ge(p_mm, count(s, h, GROUPS, G_U + g + 1))
                        if g == 0 and isinstance(s, int) and s == 0 and h == 0:
                            act.wait_ge(st_zero, 2)
                        elif g == 0:
                            act.wait_ge(u_hist, count(s, h, 1, 0))
                        for a in range(2):
                            e = 2 * g + a
                            act.activation(uraw[:, e, HIST:HIST + T], m_bank[(G_U + g) % 2][:, a * T:(a + 1) * T], ACT.Identity,
                                           bias=bcin[:, e:e + 1]).then_inc(u_raw, 1)
                        act.wait_ge(u_raw, count(s, h, E, 2 * g + 2))
                        for a in range(2):
                            e = 2 * g + a
                            ins = act.activation(u[:, h, e, :], uraw[:, e, 0:T], ACT.Identity,
                                                 scale=cols[:, C_CONVW + e * TAPS:C_CONVW + e * TAPS + 1],
                                                 bias=cols[:, C_CONVB + e:C_CONVB + e + 1])
                            ins.then_inc(u_tap, 1)
                    if i == AT_Z + 2 * g + 1:
                        act.wait_ge(p_mm, count(s, h, GROUPS, G_Z + g + 1))
                        for a in range(2):
                            e = 2 * g + a
                            act.activation(z[:, h, e, :], m_bank[(G_Z + g) % 2][:, a * T:(a + 1) * T], ACT.Identity,
                                           bias=bcin[:, E + e:E + e + 1]).then_inc(z_raw, 1)
                if i == AT_SILU:
                    act.wait_ge(z_raw, count(s, h, E, E))
                    uu = u[:, h, :, :].rearrange("p a t -> p (a t)")
                    zz = z[:, h, :, :].rearrange("p a t -> p (a t)")
                    act.activation(zz, zz, ACT.Silu).then_inc(silu_done, 1)
                    act.wait_ge(u_conv, count(s, h, 3 * E, 3 * E))
                    act.activation(uu, uu, ACT.Silu).then_inc(silu_done, 1)
                    act.preload_act_table_set("natural_log_exp_and_others")
                if i == AT_XD:
                    act.wait_ge(p_mm, count(s, h, GROUPS, G_XP + 1))
                    act.activation(xd[:, :], m_bank[G_XP % 2][:, 0:T], ACT.Copy).then_inc(xd_read, 1)
                if AT_SPLIT <= i < AT_SPLIT + SPLITS and (i - AT_SPLIT) % 3 < 2:
                    n, step = divmod(i - AT_SPLIT, 3)
                    if i == AT_SPLIT:
                        act.wait_ge(xd_read, count(s, h, 1, 1))
                    else:
                        act.wait_ge(split, count(s, h, SPLITS, i - AT_SPLIT))
                    if step == 0:
                        act.activation(xs[:, :], (xd[:, :], xr1, xr2)[n], ACT.Copy).then_inc(split, 1)
                    else:
                        act.activation((xr1, xr2)[n], xs[:, :], ACT.Identity,
                                       scale=behind[:, n:n + 1]).then_inc(split, 1)
                for g in range(E // 2 - 1):
                    softplus(s, h, g, i - AT_DT - 3 * g)

            def softplus(s, h, g, step):
                if step == 1:
                    c = count(s, h, 3 * E, 6 * g)
                    act.wait_ge(p_mm, count(s, h, GROUPS, dt_group(g) + 1))
                    for a in range(2):
                        e = 2 * g + a
                        act.activation(delta[:, e, :], m_bank[dt_group(g) % 2][:, a * T:(a + 1) * T], ACT.Identity,
                                       bias=cols[:, C_BDT + e:C_BDT + e + 1]).then_inc(sp_act, 1)
                    act.wait_ge(sp_act, c + 2)
                    again = not (isinstance(s, int) and s == 0 and h == 0 and g == 0)
                    if again:
                        act.wait_ge(sp_dve, count(s, h, E, 2 * g))
                    x2 = delta[:, 2 * g:2 * g + 2, :].rearrange("p a t -> p (a t)")
                    act.activation(spa[:, :], x2, ACT.Abs).then_inc(sp_act, 1)
                    act.wait_ge(sp_act, c + 3)
                    act.activation(spa[:, :], spa[:, :], ACT.Exp, scale=-1.0).then_inc(sp_act, 1)
                    act.wait_ge(sp_act, c + 4)
                    act.activation(spw[:, :], spa[:, :], ACT.Identity, bias=1.0).then_inc(sp_act, 1)
                    if again:
                        act.wait_ge(sp_pool, count(s, h, E, 2 * g - 1))
                    act.activation(spl[:, :], spa[:, :], ACT.Ln, bias=1.0).then_inc(sp_act, 1)

            def read_bc(s, h, np_):
                for w in range(2):
                    if not (isinstance(s, int) and s == 0 and h == 0):
                        act.wait_ge([bx_done, pr_done][w], count(s, h, SLOTS, np_ + 1 - PAIRS))
                    act.wait_ge(p_mm, count(s, h, GROUPS, G_BC + 2 * np_ + w + 1))
                    act.activation(bc[:, w, np_, :], m_bank[(G_BC + w) % 2][:, :], ACT.Copy).then_inc(bc_done, 1)

            def chunk(s, h, following=True):
                for i in range(SLOTS):
                    if i + EX_AHEAD < SLOTS:
                        exps(s, h, i + EX_AHEAD)
                    elif following:
                        exps(s + h, 1 - h, i + EX_AHEAD - SLOTS)
                    if i < BC_OVER:
                        read_bc(s, h, PAIRS - BC_OVER + i)
                    softplus(s, h, E // 2 - 1, i - AT_DT_LAST)
                    if following:
                        pieces(s + h, 1 - h, i)
                        if i >= AT_BC:
                            read_bc(s + h, 1 - h, i - AT_BC)

            def iteration(s, following=True):
                chunk(s, 0)
                chunk(s, 1, following)

            for i in range(SLOTS):
                pieces(0, 0, i)
                if i >= AT_BC:
                    read_bc(0, 0, i - AT_BC)
            for i in range(EX_AHEAD):
                exps(0, 0, i)
            iteration(0)
            with act.Fori(1, n_sup - 2) as s:
                iteration(s)
            iteration(n_sup - 2)
            iteration(n_sup - 1, following=False)

        @block.vector
        def _(dve):
            def stats_tok(q, t, landed):
                dve.wait_ge(x_landed[t], landed)
                for kt in range(KG):
                    dve.bn_stats(stats[:, t, kt, :], xtok[t][:, kt, :]).then_inc(s_stats, 1)
                dve.wait_ge(s_stats, q * KG + KG)
                dve.memset(spare[:, :], 0.0)
                for kt in range(KG):
                    ins = dve.bn_aggr(mv[:, t, kt, :], stats[:, t, kt, :])
                ins.then_inc(s_var, 1)

            def apply_tok(q, t):
                dve.wait_ge(s_rstd, q * 2 + 2)
                for kt in range(KG):
                    dve.tensor_scalar(xtok[t][:, kt, :], xtok[t][:, kt, :], mv[:, t, kt, 0:1], rtok[:, t, kt:kt + 1],
                                      ALU.subtract, ALU.mult).then_inc(s_xn, 1)

            def read_support(q, t, stored):
                dve.wait_ge(s_mm, q + 1)
                if stored is not None:
                    dve.wait_ge(s_stored[t], stored)
                for b in range(2):
                    src = [g_bank, y_bank][t][b]
                    dve.tensor_copy(sout[t].rearrange("p a f -> p (a f)")[:, b * 512:b * 512 + 512],
                                    src[:, :]).then_inc(s_out, 1)

            stats_tok(0, 0, 16)
            apply_tok(0, 0)
            stats_tok(1, 1, 16)
            apply_tok(1, 1)
            stats_tok(2, 0, 32)
            apply_tok(2, 0)
            read_support(0, 0, None)
            stats_tok(3, 1, 32)
            apply_tok(3, 1)
            read_support(1, 1, None)
            stats_tok(4, 0, 48)
            apply_tok(4, 0)
            read_support(2, 0, 16)
            with dve.Fori(2, n_grp // 2 - 1) as j:
                stats_tok(j * 2 + 1, 1, j * 16 + 16)
                apply_tok(j * 2 + 1, 1)
                read_support(j * 2 - 1, 1, j * 16 - 16)
                stats_tok(j * 2 + 2, 0, j * 16 + 32)
                apply_tok(j * 2 + 2, 0)
                read_support(j * 2, 0, j * 16)
            stats_tok(n_grp - 1, 1, n_grp // 2 * 16)
            apply_tok(n_grp - 1, 1)
            read_support(n_grp - 3, 1, 8 * (n_grp - 4))
            read_support(n_grp - 2, 0, 8 * (n_grp - 2))
            read_support(n_grp - 1, 1, 8 * (n_grp - 2))

            dve.wait_ge(w_small, SP_SMALL)
            dve.wait_ge(st_zero, 2)

            def read_gnn(s):
                dve.wait_ge(adj_used, s * n_ld + n_ld)
                dve.wait_ge(xin_landed, s * 16 + 16)
                if not (isinstance(s, int) and s == 0):
                    dve.wait_ge(held, s * 2)
                    dve.wait_ge(ln_xc, s * 2)
                for f in range(FH):
                    dve.scalar_tensor_tensor(x1n[:, f, :], g_bank[f][:, :], cols[:, C_GB + f:C_GB + f + 1],
                                             xin[:, f, :], ALU.add, ALU.add).then_inc(g_read, 1)

            def scan_inputs(s, h, i):
                dve.wait_ge(exp_done, count(s, h, SLOTS, i + 1))
                dve.wait_ge(bx_done, count(s, h, SLOTS, i + 1))
                first = isinstance(s, int) and s == 0 and h == 0
                if not (first and i < 2):
                    dve.wait_ge(pr_done, count(s, h, SLOTS, i - 1))
                    dve.wait_ge(st_done, count(s, h, SLOTS, i - 1))

            def unit_scan(s, h, i, a):
                d, np_ = divmod(i, PAIRS)
                n = 2 * np_ + a
                dve.tensor_tensor_scan(h_bank[i % 2][:, a * T:(a + 1) * T], ex[:, i % EX_RING, a * T:(a + 1) * T],
                                       bx[:, i % BX_RING, a * T:(a + 1) * T], state[:, d, n:n + 1],
                                       ALU.mult, ALU.add).then_inc(scan_done, 1)

            def unit_mult(s, h, i):
                d, np_ = divmod(i, PAIRS)
                dve.wait_ge(scan_done, count(s, h, 2 * SLOTS, 2 * i + 2))
                if d == 0:
                    dve.wait_ge(bc_done, count(s, h, 2 * PAIRS, 2 * np_ + 2))
                if not (isinstance(s, int) and count(s, h, SLOTS, i) < PR_RING):
                    dve.wait_ge(sum_done, count(s, h, SLOTS, i - PR_RING + 1))
                dve.tensor_tensor(pr[:, i % PR_RING, :], h_bank[i % 2][:, :], bc[:, 1, np_, :], ALU.mult).then_inc(pr_done, 1)
                last = h_bank[i % 2][:, :].rearrange("p (a t) -> p a t", a=2)[:, :, T - 1]
                dve.tensor_copy(state[:, d, 2 * np_:2 * np_ + 2], last).then_inc(st_done, 1)

            def add_skip(s, h, d):
                dve.wait_ge(sum_done, count(s, h, SLOTS, (d + 1) * PAIRS))
                if d == 0 and not (isinstance(s, int) and s == 0 and h == 0):
                    dve.wait_ge(o_mm, count(s, h, 1, 0))
                if not (isinstance(s, int) and s == 0 and h == 0 and d == 0):
                    dve.wait_ge(y_done, count(s, h, E, d))
                dve.scalar_tensor_tensor(ytmp[:, :], u[:, h, d, :], cols[:, C_D + d:C_D + d + 1], y_bank[d % 2][:, 0:T],
                                         ALU.mult, ALU.add).then_inc(y_free, 1)

            def gate(s, h, d):
                dve.wait_ge(y_free, count(s, h, E, d + 1))
                dve.tensor_tensor(y2[:, d, :], ytmp[:, :], z[:, h, d, :], ALU.mult).then_inc(y_done, 1)

            def finish(s, h):
                dve.wait_ge(o_mm, count(s, h, 1, 1))
                if not (isinstance(s, int) and s == 0 and h == 0):
                    dve.wait_ge(o_stored, count(s, h, 16, 0))
                dve.tensor_tensor(ob[:, :, :], m_bank[G_O % 2][:, :].rearrange("p (f t) -> p f t", f=FH), hold[:, h, :, :],
                                  ALU.add).then_inc(o_free, 1)

            def pieces(s, h, i):
                half = slice(h * T, h * T + T)
                if i == AT_MEAN + 1:
                    dve.wait_ge(p_mm, count(s, h, GROUPS, G_MEAN + 1))
                    if not (isinstance(s, int) and s == 0 and h == 0):
                        dve.wait_ge(split, count(s, h, SPLITS, 0))
                    m = m_bank[G_MEAN % 2][:, 0:T].unsqueeze(1).to_broadcast([P, FH, T])
                    dve.tensor_tensor(xc[:, :, :], x1n[:, :, half], m, ALU.subtract).then_inc(ln_xc, 1)
                if i == AT_XN:
                    dve.wait_ge(ln_rstd, count(s, h, 1, 1))
                    r = rstd[:, :].unsqueeze(1).to_broadcast([P, FH, T])
                    dve.tensor_tensor(xc[:, :, :], xc[:, :, :], r, ALU.mult).then_inc(ln_xn, 1)
                for g in range(E // 2):
                    first = AT_TAPS + 2 * g if g < E // 2 - 1 else AT_SILU
                    if i == first:
                        dve.wait_ge(u_tap, count(s, h, E, 2 * g + 2))
                    if i in (first, first + 1):
                        for n in range(3 * (i - first), 3 * (i - first) + 3):
                            j, e = 1 + n // 2, 2 * g + n % 2
                            if n >= 2:
                                dve.wait_ge(u_conv, count(s, h, 3 * E, 6 * g + n - 1))
                            w = C_CONVW + e * TAPS + j
                            dve.scalar_tensor_tensor(u[:, h, e, :], uraw[:, e, j:j + T], cols[:, w:w + 1],
                                                     u[:, h, e, :], ALU.mult, ALU.add).then_inc(u_conv, 1)

            def correct(s, h, g):
                dve.wait_ge(sp_act, count(s, h, 3 * E, 6 * g + 5))
                dve.scalar_tensor_tensor(spw[:, :], spw[:, :], -1.0, spa[:, :], ALU.add,
                                         ALU.subtract).then_inc(sp_dve, 1)

            def rectify(s, h, g):
                dve.wait_ge(sp_dve, count(s, h, E, 2 * g + 1))
                x2 = delta[:, 2 * g:2 * g + 2, :].rearrange("p a t -> p (a t)")
                dve.scalar_tensor_tensor(x2, x2, 0.0, spw[:, :], ALU.max, ALU.subtract).then_inc(sp_dve, 1)

            def in_two_steps(s, h, i, step, before, following):
                for g in range(E // 2):
                    if g == E // 2 - 1 and i == AT_DT_LAST + 3 + LAST_SLACK:
                        (correct, rectify)[step](s, h, g)
                    elif g < E // 2 - 1 and i == AT_DT + 3 * g + 3 and following:
                        (correct, rectify)[step](s + h, 1 - h, g)
                if i % PAIRS == AT_GATE:
                    if i > PAIRS:
                        (add_skip, gate)[step](s, h, i // PAIRS - 1)
                    elif before:
                        (add_skip, gate)[step](s - 1 + h, 1 - h, E - 1)

            def chunk(s, h, before=True, following=True, gnn=True):
                for i in range(SLOTS):
                    scan_inputs(s, h, i)
                    unit_scan(s, h, i, 0)
                    if i > 0:
                        unit_mult(s, h, i - 1)
                    elif before:
                        unit_mult(s - 1 + h, 1 - h, SLOTS - 1)
                    in_two_steps(s, h, i, 0, before, following)
                    unit_scan(s, h, i, 1)
                    in_two_steps(s, h, i, 1, before, following)
                    if i == AT_STORE and before:
                        finish(s - 1 + h, 1 - h)
                    if i == AT_GREAD and h == 1 and gnn:
                        read_gnn(s + 1)
                    if following:
                        pieces(s + h, 1 - h, i)

            def iteration(s, before=True, following=True, gnn=True):
                chunk(s, 0, before=before)
                chunk(s, 1, following=following, gnn=gnn)

            read_gnn(0)
            for i in range(SLOTS):
                pieces(0, 0, i)
                for g in range(E // 2 - 1):
                    if i == AT_DT + 3 * g + 3:
                        correct(0, 0, g)
                        rectify(0, 0, g)
            iteration(0, before=False)
            with dve.Fori(1, n_sup - 2) as s:
                iteration(s)
            iteration(n_sup - 2)
            iteration(n_sup - 1, following=False, gnn=False)
            unit_mult(n_sup - 1, 1, SLOTS - 1)
            add_skip(n_sup - 1, 1, E - 1)
            gate(n_sup - 1, 1, E - 1)
            finish(n_sup - 1, 1)

        @block.tensor
        def _(pe):
            pe.wait_ge(w_small, SP_SMALL)
            pe.wait_ge(consts_set, 3)

            def transposes(q, t, free):
                pe.wait_ge(s_xn, q * KG + KG)
                if free is not None:
                    pe.wait_ge(s_trc, free)
                for f in range(FH):
                    for kt in range(KG):
                        ins = pe.transpose([m_bank, h_bank][t][f][:, kt * P:(kt + 1) * P],
                                           xtok[t][:, kt, f * P:(f + 1) * P], ident[:, :])
                ins.then_inc(s_tr, 1)

            def products(q, t, free):
                pe.wait_ge(s_trc, q * 2 + 2)
                if free is not None:
                    pe.wait_ge(s_out, free)
                for kt in range(KG):
                    dst = [g_bank, y_bank][t][kt // 2]
                    for f in range(FH):
                        ins = pe.matmul(dst[:, kt % 2 * F:kt % 2 * F + F], xnt[t][:, f, kt * P:(kt + 1) * P],
                                        wg[:, f, :], start=(f == 0), stop=(f == FH - 1))
                ins.then_inc(s_mm, 1)

            transposes(0, 0, None)
            transposes(1, 1, None)
            products(0, 0, None)
            transposes(2, 0, 2)
            products(1, 1, None)
            with pe.Fori(1, n_grp // 2 - 1) as j:
                transposes(j * 2 + 1, 1, j * 4)
                products(j * 2, 0, j * 4 - 2)
                transposes(j * 2 + 2, 0, j * 4 + 2)
                products(j * 2 + 1, 1, j * 4)
            transposes(n_grp - 1, 1, 2 * (n_grp - 2))
            products(n_grp - 2, 0, 2 * (n_grp - 3))
            products(n_grp - 1, 1, 2 * (n_grp - 2))

            pe.wait_ge(w_big, SP_BIG)
            for n in range(FOLDS):
                dst = [m_bank, h_bank][n // 2 % 2][n % 2]
                if n < 4:
                    pe.wait_ge(s_trc, 2 * n_grp)
                else:
                    pe.wait_ge(fold_out, n - 3)
                if n < FH * 4:
                    f, c = divmod(n, 4)
                    for k in range(DMT):
                        ins = pe.matmul(dst[:, :], wf1[:, k, f * P:(f + 1) * P], win[:, k, c * 512:(c + 1) * 512],
                                        start=(k == 0), stop=(k == DMT - 1))
                elif n < FOLDS - 1:
                    for a in range(2):
                        d = 2 * (n - FH * 4) + a
                        for k in range(DMT):
                            ins = pe.matmul(dst[:, a * F:(a + 1) * F], wout[:, k, d * P:(d + 1) * P], wf2[:, k, :],
                                            start=(k == 0), stop=(k == DMT - 1))
                else:
                    for e in range(2 * E):
                        for k in range(DMT):
                            ins = pe.matmul(dst[:, e:e + 1], win[:, k, e * P:(e + 1) * P],
                                            cols[:, C_B1 + k:C_B1 + k + 1], start=(k == 0), stop=(k == DMT - 1))
                ins.then_inc(fold_mm, 1)

            def gnn(s, lo, hi):
                for m in range(lo, hi):
                    kt, f = divmod(m, FH)
                    r = kt // KL
                    if m == 0:
                        if isinstance(s, int) and s == 0:
                            pe.wait_ge(s_out, 2 * n_grp)
                        else:
                            pe.wait_ge(g_read, s * FH)
                    if kt % KL == 0 and f == 0:
                        per = n_ld // RING * 32
                        pe.wait_ge(adj_landed[r % RING], s * per + 32 * (r // RING + 1))
                    ins = pe.matmul(g_bank[f][:, :],
                                    sup_sb[:, r % RING, kt % KL * F + f * P:kt % KL * F + (f + 1) * P],
                                    adj_sb[:, r % RING, kt % KL * SUP:(kt % KL + 1) * SUP],
                                    start=(kt == 0), stop=(kt == n_ld * KL - 1))
                    if kt % KL == KL - 1 and f == FH - 1:
                        ins.then_inc(adj_used, 1)

            def sums(s, h, i):
                d, np_ = divmod(i, PAIRS)
                first = isinstance(s, int) and s == 0 and h == 0
                if is_halved(i):
                    pe.wait_ge(pr_halved, count(s, h, halved(SLOTS), halved(i + 1)))
                else:
                    pe.wait_ge(pr_done, count(s, h, SLOTS, i + 1))
                if np_ == 0 and not (first and d < 2):
                    pe.wait_ge(y_free, count(s, h, E, d - 1))
                parts = 1 if is_halved(i) else 2
                for a in range(parts):
                    ins = pe.matmul(y_bank[d % 2][:, 0:T], ident[:, :], pr[:, i % PR_RING, a * T:(a + 1) * T],
                                    start=(np_ == 0 and a == 0), stop=(np_ == PAIRS - 1 and a == parts - 1))
                ins.then_inc(sum_done, 1)

            def out_product(s, h, j, groups=2):
                if j == 0:
                    pe.wait_ge(y_done, count(s, h, E, E))
                    pe.wait_ge(bc_done, count(s, h, 2 * PAIRS, 2 * PAIRS * groups))
                for n in range(4 * j, 4 * j + 4):
                    f, d = divmod(n, E)
                    ins = pe.matmul(m_bank[G_O % 2][:, f * T:(f + 1) * T], wo[:, d, f * P:(f + 1) * P], y2[:, d, :],
                                    start=(d == 0), stop=(d == E - 1))
                if j == 3:
                    ins.then_inc(o_mm, 1)

            def pieces(s, h, i, before):
                half = slice(h * T, h * T + T)

                if i == AT_MEAN:
                    if isinstance(s, int) and s == 0 and h == 0:
                        pe.wait_ge(fold_out, FOLDS)
                    else:
                        pe.wait_ge(sp_act, count(s, h, 3 * E, -4))
                    pe.wait_ge(g_read, s * FH + FH)
                    for f in range(FH):
                        ins = pe.matmul(m_bank[G_MEAN % 2][:, 0:T], ones[:, :], x1n[:, f, half], start=(f == 0), stop=(f == FH - 1))
                    ins.then_inc(p_mm, 1)
                if i == AT_VAR:
                    pe.wait_ge(ln_sq, count(s, h, 1, 1))
                    if before:
                        pe.wait_ge(o_free, count(s - 1, h, 1, 1))
                    for f in range(FH):
                        ins = pe.matmul(m_bank[G_VAR % 2][:, 0:T], ones[:, :], sq[:, f, :], start=(f == 0), stop=(f == FH - 1))
                    ins.then_inc(p_mm, 1)
                for g in range(E // 2 - 1):
                    if i == AT_DT + 3 * g:
                        dt_product(s, h, g)
                for g in range(E // 2):
                    for at, base, off in ((AT_U, G_U, 0), (AT_Z, G_Z, E)):
                        if i == at + 2 * g:
                            if off == 0 and g == 0:
                                pe.wait_ge(ln_xn, count(s, h, 1, 1))
                            elif off == 0 and g > 1:
                                pe.wait_ge(u_raw, count(s, h, E, 2 * g - 2))
                            elif off and g < 2:
                                pe.wait_ge(u_raw, count(s, h, E, E + 2 * g - 2))
                            elif off:
                                pe.wait_ge(z_raw, count(s, h, E, 2 * g - 2))
                            for a in range(2):
                                e = off + 2 * g + a
                                for f in range(FH):
                                    ins = pe.matmul(m_bank[(base + g) % 2][:, a * T:(a + 1) * T], wc[:, f, e * P:(e + 1) * P], xc[:, f, :],
                                                    start=(f == 0), stop=(f == FH - 1))
                            ins.then_inc(p_mm, 1)
                if AT_XP <= i < AT_XP + 4:
                    if i == AT_XP:
                        pe.wait_ge(z_raw, count(s, h, E, E))
                        pe.wait_ge(silu_done, count(s, h, 2, 2))
                    for e in (2 * (i - AT_XP), 2 * (i - AT_XP) + 1):
                        ins = pe.matmul(m_bank[G_XP % 2][:, 0:T], wxp[:, e, :], u[:, h, e, :], start=(e == 0), stop=(e == E - 1))
                    if i == AT_XP + 3:
                        ins.then_inc(p_mm, 1)

            def dt_product(s, h, g):
                if g < 2:
                    pe.wait_ge(xd_read, count(s, h, 1, 1))
                elif g == 2:
                    pe.wait_ge(sp_act, count(s, h, 3 * E, 2))
                else:
                    pe.wait_ge(bc_done, count(s, h, 2 * PAIRS, 2 * PAIRS - 1))
                for a in range(2):
                    e = 2 * g + a
                    ins = pe.matmul(m_bank[dt_group(g) % 2][:, a * T:(a + 1) * T], wdt[P - R:P, e * P:(e + 1) * P],
                                    xd[P - R:P, :], start=True, stop=True)
                ins.then_inc(p_mm, 1)

            def spread(s, h, np_, w):
                if np_ == 0 and w == 0:
                    pe.wait_ge(split, count(s, h, SPLITS, SPLITS))
                if np_ == 0:
                    pe.wait_ge(sp_act, count(s, h, 3 * E, 6 * (w + 1) + 2))
                else:
                    pe.wait_ge(bc_done, count(s, h, 2 * PAIRS, 2 * np_ + w - 1))
                for a in range(2):
                    row = w * NS + 2 * np_ + a
                    ins = pe.matmul(m_bank[(G_BC + w) % 2][:, a * T:(a + 1) * T], pick[:, row:row + 1].to_broadcast([96, P]),
                                    xs[0:96, :], start=True, stop=True)
                ins.then_inc(p_mm, 1)

            def chunk(s, h, before=True, following=True, product=True, begin=True):
                for i in range(SLOTS):
                    for w in range(2):
                        if i < BC_OVER:
                            spread(s, h, PAIRS - BC_OVER + i, w)
                        elif i >= AT_BC and following:
                            spread(s + h, 1 - h, i - AT_BC, w)
                    if i == AT_DT_LAST:
                        dt_product(s, h, E // 2 - 1)
                    if following:
                        pieces(s + h, 1 - h, i, before)
                    if before and AT_OUT <= i < AT_OUT + 4:
                        out_product(s - 1 + h, 1 - h, i - AT_OUT)
                    if i >= SUM_LAG:
                        sums(s, h, i - SUM_LAG)
                    elif before:
                        sums(s - 1 + h, 1 - h, SLOTS - SUM_LAG + i)
                    if product:
                        if h == 0:
                            at = SLOTS - AT_G + i
                            gnn(s + 1, g_ends[at - 1], g_ends[at])
                        elif i < AT_GEND:
                            at = 2 * SLOTS - AT_G + i
                            gnn(s + 1, g_ends[at - 1], g_ends[at])
                        elif i >= AT_G and begin:
                            at = i - AT_G
                            gnn(s + 2, g_ends[at - 1] if at else 0, g_ends[at])

            def iteration(s, before=True, following=True, product=True, begin=True):
                chunk(s, 0, before=before, product=product)
                chunk(s, 1, following=following, product=product, begin=begin)

            gnn(0, 0, n_mm)
            for i in range(SLOTS):
                pieces(0, 0, i, False)
                for w in range(2):
                    if i >= AT_BC:
                        spread(0, 0, i - AT_BC, w)
                gnn(1, i * g_first // SLOTS, (i + 1) * g_first // SLOTS)
            iteration(0, before=False)
            with pe.Fori(1, n_sup - 2) as s:
                iteration(s)
            iteration(n_sup - 2, begin=False)
            iteration(n_sup - 1, following=False, product=False)
            for i in range(SUM_LAG):
                sums(n_sup - 1, 1, SLOTS - SUM_LAG + i)
            for j in range(4):
                out_product(n_sup - 1, 1, j, groups=1)


def kernel(**inputs):
    import numpy as np
    import ml_dtypes
    import concourse.bacc as bacc
    from concourse.bass_utils import run_bass_kernel_spmd

    a = {k: np.asarray(v) for k, v in inputs.items()}
    w = {k[3:]: v for k, v in a.items() if k.startswith("L0_")}
    n = a["x"].shape[0]
    sups, grps, loads = n // SUP, n // (KG * P), n // (KL * P)

    def tiles(v):
        v = v.reshape(v.shape[0] // P, P, *v.shape[1:])
        return np.ascontiguousarray(np.moveaxis(v, 0, 1))

    def flat(v):
        return tiles(v).reshape(P, -1)

    xp = w["ffn_W_xproj"]
    xp4 = np.concatenate([xp[R:], xp[R:], xp[R:], xp[:R]], axis=0)
    arrays = {
        "adj_g": np.ascontiguousarray(
            a["adj"].reshape(sups, SUP, loads, KL, P).transpose(0, 2, 4, 3, 1)).reshape(sups, loads, P, KL * SUP),
        "x_tok": np.ascontiguousarray(a["x"].reshape(grps, KG, P, F).transpose(0, 2, 1, 3)).reshape(grps, P, KG * F),
        "x_fm": np.ascontiguousarray(a["x"].reshape(sups, SUP, FH, P).transpose(0, 3, 2, 1)),
        "gnn_w": tiles(w["gnn_weight"]),
        "w_fc1": tiles(w["ffn_W_fc1"]),
        "w_in_t": tiles(w["ffn_W_in"].T),
        "w_out": tiles(w["ffn_W_out"]),
        "w_fc2_t": tiles(w["ffn_W_fc2"].T),
        "w_xp_t": tiles(xp4.T),
        "w_dt_t": np.ascontiguousarray(w["ffn_W_dt"].T),
        "columns": np.concatenate([flat(w[k]) for k in (
            "ffn_conv_w", "ffn_conv_b", "ffn_D", "ffn_b_dt", "gnn_bias", "ffn_b_fc2", "ffn_b_fc1", "ffn_A_log")], axis=1),
        "ident_in": np.eye(P, dtype=np.float32),
        "behind_in": (np.arange(P)[:, None] >= np.array([[32, 64]])).astype(np.float32),
        "pick_in": np.tile(np.eye(R, dtype=np.float32), (3, 1)).astype(ml_dtypes.bfloat16),
    }
    nc = bacc.Bacc("TRN2", target_bir_lowering=False, num_devices=1, dynamic_dma_scratch_size=1024)
    aps = {k: nc.dram_tensor(k, v.shape, mybir.dt.from_np(v.dtype), kind="ExternalInput").ap() for k, v in arrays.items()}
    support = nc.dram_tensor("support", (grps, P, KG * F), F32, kind="Internal").ap()
    out = nc.dram_tensor("out", (2 * sups, P, FH, T), F32, kind="ExternalOutput").ap()
    graph_mamba_program(nc, **aps, support=support, out=out)
    got = run_bass_kernel_spmd(nc, [arrays], core_ids=[0]).results[0]["out"]
    return np.ascontiguousarray(got.transpose(0, 3, 2, 1)).reshape(n, F)
```
